# Optimizing a Trainium2 kernel written in Bass

```python
import numpy as np
import jax
import jax.numpy as jnp

def _softmax(x, axis=-1):
    return jax.nn.softmax(x, axis=axis)

def _gelu(x):
    return jax.nn.gelu(x, approximate=True)

def _silu(x):
    return jax.nn.silu(x)

def _sigmoid(x):
    return jax.nn.sigmoid(x)

def _layernorm(x, axis=-1, eps=1e-05):
    m = jnp.mean(x, axis=axis, keepdims=True)
    v = jnp.var(x, axis=axis, keepdims=True)
    return (x - m) / jnp.sqrt(v + eps)

def _scatter_add(tgt, idx, src, axis=0):
    return tgt.at[idx].add(src)

def _segment_sum(src, seg, n):
    return jax.ops.segment_sum(src, seg, n)
kernel_name = 'mk_cond_seq_d4_seqx_r8_fda9fe'

def setup_inputs(seed: int=0):
    np.random.seed(seed)
    _w = jnp.asarray

    def _rec_inputs():
        import jax
        import jax.numpy as jnp
        _rk = jax.random.key(seed)
        x = 7.22e-05 + 1 * jax.random.normal(jax.random.fold_in(_rk, 1), (2, 512, 128), jnp.float32)
        _lenS = 512 - jax.random.randint(jax.random.fold_in(_rk, 7), (2,), 0, max(1, 512 // 4) + 1, jnp.int32)
        _lenS2 = 512 - jax.random.randint(jax.random.fold_in(_rk, 8), (2,), 0, max(1, 512 // 4) + 1, jnp.int32)
        cond_1024 = 0.0061147 + 1.02565 * jax.random.normal(jax.random.fold_in(_rk, 11), (2, 128), jnp.float32)
        itok_BxSx2_0_63 = jax.random.randint(jax.random.fold_in(_rk, 12), (2, 512, 2), 0, 64, jnp.int32)
        _validS = jnp.arange(512)[None, :] < _lenS[:, None]
        _validS2 = jnp.arange(512)[None, :] < _lenS2[:, None]
        _causal = jnp.tril(jnp.ones((512, 512), dtype=bool))
        mask_BxS_bk0 = jnp.logical_not(jnp.broadcast_to(_validS[:, :], (2, 512)))
        return (x, cond_1024, itok_BxSx2_0_63, mask_BxS_bk0)
    x, cond_1024, itok_BxSx2_0_63, mask_BxS_bk0 = _rec_inputs()

    def _L0_cond_setup():
        import jax, jax.numpy as jnp
        import numpy as np
        D_MODEL = 128
        NHEAD = 16
        HEAD_DIM = D_MODEL // NHEAD
        D_FF = 512
        EPS = 1e-05

        def _layernorm(x):
            mu = jnp.mean(x, axis=-1, keepdims=True)
            var = jnp.var(x, axis=-1, keepdims=True)
            return (x - mu) * jax.lax.rsqrt(var + EPS)
        key = jax.random.key(seed)
        ks = jax.random.split(key, 16)
        B, N = (4, 256)
        s = 0.02
        inp = {'x': jax.random.normal(ks[0], (B, N, D_MODEL), jnp.float32), 'c': jax.random.normal(ks[1], (B, D_MODEL), jnp.float32), 'W_ada': jax.random.normal(ks[2], (D_MODEL, 6 * D_MODEL), jnp.float32) * s, 'b_ada': jnp.zeros((6 * D_MODEL,), jnp.float32), 'Wq': jax.random.normal(ks[3], (D_MODEL, D_MODEL), jnp.float32) * s, 'bq': jnp.zeros((D_MODEL,), jnp.float32), 'Wk': jax.random.normal(ks[4], (D_MODEL, D_MODEL), jnp.float32) * s, 'bk': jnp.zeros((D_MODEL,), jnp.float32), 'Wv': jax.random.normal(ks[5], (D_MODEL, D_MODEL), jnp.float32) * s, 'bv': jnp.zeros((D_MODEL,), jnp.float32), 'Wo': jax.random.normal(ks[6], (D_MODEL, D_MODEL), jnp.float32) * s, 'bo': jnp.zeros((D_MODEL,), jnp.float32), 'W1': jax.random.normal(ks[7], (D_MODEL, D_FF), jnp.float32) * s, 'b1': jnp.zeros((D_FF,), jnp.float32), 'W2': jax.random.normal(ks[8], (D_FF, D_MODEL), jnp.float32) * s, 'b2': jnp.zeros((D_MODEL,), jnp.float32)}
        return inp
    _L0_cond_all = _L0_cond_setup()
    _L0_cond_in = {k: v for k, v in _L0_cond_all.items() if k in ('W_ada', 'b_ada', 'Wq', 'bq', 'Wk', 'bk', 'Wv', 'bv', 'Wo', 'bo', 'W1', 'b1', 'W2', 'b2')}
    del _L0_cond_all

    def _L1_cond_setup():
        import jax, jax.numpy as jnp
        import numpy as np
        EPS = 1e-06
        ROPE_BASE = 100.0

        def layernorm(x):
            mu = jnp.mean(x, axis=-1, keepdims=True)
            var = jnp.var(x, axis=-1, keepdims=True)
            return (x - mu) / jnp.sqrt(var + EPS)

        def modulate(x, shift, scale):
            return x * (1.0 + scale[:, None, :]) + shift[:, None, :]

        def rope1d(t, pos):
            d = t.shape[-1]
            inv_freq = 1.0 / ROPE_BASE ** (jnp.arange(0, d, 2, dtype=jnp.float32) / d)
            ang = pos[:, None, :, None] * inv_freq
            ang = jnp.concatenate([ang, ang], axis=-1)
            cos, sin = (jnp.cos(ang), jnp.sin(ang))
            t1, t2 = (t[..., :d // 2], t[..., d // 2:])
            rot = jnp.concatenate([-t2, t1], axis=-1)
            return t * cos + rot * sin

        def rope2d(t, positions):
            hd = t.shape[-1]
            pos = positions.astype(jnp.float32)
            ty = rope1d(t[..., :hd // 2], pos[..., 0])
            tx = rope1d(t[..., hd // 2:], pos[..., 1])
            return jnp.concatenate([ty, tx], axis=-1)
        key = jax.random.key(seed)
        ks = jax.random.split(key, 13)
        B, N, D, Hm = (2, 256, 128, 512)
        s = lambda k, shp, fan: jax.random.normal(k, shp, jnp.float32) * fan ** (-0.5)
        return {'x': jax.random.normal(ks[0], (B, N, D), jnp.float32), 'c': jax.random.normal(ks[1], (B, D), jnp.float32), 'positions': jax.random.randint(ks[2], (B, N, 2), 0, 64, jnp.int32), 'qkv_w': s(ks[3], (D, 3 * D), D), 'qkv_b': jnp.zeros((3 * D,), jnp.float32), 'proj_w': s(ks[4], (D, D), D), 'proj_b': jnp.zeros((D,), jnp.float32), 'fc1_w': s(ks[5], (D, Hm), D), 'fc1_b': jnp.zeros((Hm,), jnp.float32), 'fc2_w': s(ks[6], (Hm, D), Hm), 'fc2_b': jnp.zeros((D,), jnp.float32), 'ada_w': s(ks[7], (D, 6 * D), D), 'ada_b': jnp.zeros((6 * D,), jnp.float32)}
    _L1_cond_all = _L1_cond_setup()
    _L1_cond_in = {k: v for k, v in _L1_cond_all.items() if k in ('qkv_w', 'qkv_b', 'proj_w', 'proj_b', 'fc1_w', 'fc1_b', 'fc2_w', 'fc2_b', 'ada_w', 'ada_b')}
    del _L1_cond_all

    def _L2_cond_setup():
        import jax, jax.numpy as jnp
        import numpy as np
        B, L, D, NH, MLP = (4, 256, 128, 16, 512)
        KD = D // NH
        EPS = 1e-05

        def layer_norm(x, scale=None):
            mu = jnp.mean(x, axis=-1, keepdims=True)
            var = jnp.var(x, axis=-1, keepdims=True)
            y = (x - mu) * jax.lax.rsqrt(var + EPS)
            return y * scale if scale is not None else y

        def rotary_pos_emb(x):
            dim, seq = (x.shape[-1], x.shape[-2])
            inv_freqs = 10000.0 ** (-jnp.arange(0, dim, 2, dtype=jnp.float32) / dim)
            grid = jnp.arange(seq, dtype=jnp.float32)[:, None] * inv_freqs[None, :]
            sin = jnp.repeat(jnp.sin(grid), 2, axis=-1)
            cos = jnp.repeat(jnp.cos(grid), 2, axis=-1)
            x1, x2 = (x[..., ::2], x[..., 1::2])
            xs = jnp.stack([-x2, x1], axis=-1).reshape(x.shape)
            return x * cos + xs * sin
        key = jax.random.key(seed)
        ks = jax.random.split(key, 11)

        def lin(k, fan_in, fan_out):
            return jax.random.normal(k, (fan_in, fan_out), jnp.float32) / np.sqrt(fan_in)
        return {'x': jax.random.normal(ks[0], (B, L, D), jnp.float32), 't_emb': jax.random.normal(ks[1], (B, 1, D), jnp.float32), 'w_scale': lin(ks[2], D, D), 'w_offset': lin(ks[3], D, D), 'wq': lin(ks[4], D, D), 'wk': lin(ks[5], D, D), 'wv': lin(ks[6], D, D), 'wo': lin(ks[7], D, D), 'mlp_ln_scale': jnp.ones((D,), jnp.float32), 'w1': lin(ks[8], D, MLP), 'w2': lin(ks[9], MLP, D)}
    _L2_cond_all = _L2_cond_setup()
    _L2_cond_in = {k: v for k, v in _L2_cond_all.items() if k in ('w_scale', 'w_offset', 'wq', 'wk', 'wv', 'wo', 'mlp_ln_scale', 'w1', 'w2')}
    del _L2_cond_all

    def _L3_cond_setup():
        import jax, jax.numpy as jnp
        import numpy as np
        B, L, D = (8, 256, 128)
        FF_MULT = 2
        EPS = 1e-06

        def _layernorm(x):
            mu = jnp.mean(x, axis=-1, keepdims=True)
            var = jnp.mean(jnp.square(x - mu), axis=-1, keepdims=True)
            return (x - mu) / jnp.sqrt(var + EPS)

        def _ssm_fallback(u, w1, b1, w2, b2):
            h = jax.nn.gelu(u @ w1 + b1, approximate=False)
            return h @ w2 + b2
        key = jax.random.key(seed)
        ks = jax.random.split(key, 20)
        s = 0.02
        inp = {'x': jax.random.normal(ks[0], (B, L, D), jnp.float32), 't': jax.random.normal(ks[1], (B, D), jnp.float32), 'mask': jax.random.randint(ks[2], (B, L), 0, 2) > 0, 'ada_w': jax.random.normal(ks[3], (D, 3 * D), jnp.float32) * s, 'ada_b': jnp.zeros((3 * D,), jnp.float32), 'ssm_w1': jax.random.normal(ks[4], (D, D), jnp.float32) * s, 'ssm_b1': jnp.zeros((D,), jnp.float32), 'ssm_w2': jax.random.normal(ks[5], (D, D), jnp.float32) * s, 'ssm_b2': jnp.zeros((D,), jnp.float32), 'bwd_w1': jax.random.normal(ks[6], (D, D), jnp.float32) * s, 'bwd_b1': jnp.zeros((D,), jnp.float32), 'bwd_w2': jax.random.normal(ks[7], (D, D), jnp.float32) * s, 'bwd_b2': jnp.zeros((D,), jnp.float32), 'ffada_w': jax.random.normal(ks[8], (D, 3 * D), jnp.float32) * s, 'ffada_b': jnp.zeros((3 * D,), jnp.float32), 'ff_w1': jax.random.normal(ks[9], (D, FF_MULT * D), jnp.float32) * s, 'ff_b1': jnp.zeros((FF_MULT * D,), jnp.float32), 'ff_w2': jax.random.normal(ks[10], (FF_MULT * D, D), jnp.float32) * s, 'ff_b2': jnp.zeros((D,), jnp.float32)}
        return inp
    _L3_cond_all = _L3_cond_setup()
    _L3_cond_in = {k: v for k, v in _L3_cond_all.items() if k in ('ada_w', 'ada_b', 'ssm_w1', 'ssm_b1', 'ssm_w2', 'ssm_b2', 'bwd_w1', 'bwd_b1', 'bwd_w2', 'bwd_b2', 'ffada_w', 'ffada_b', 'ff_w1', 'ff_b1', 'ff_w2', 'ff_b2')}
    del _L3_cond_all
    return {'x': x, 'cond_1024': cond_1024, 'itok_BxSx2_0_63': itok_BxSx2_0_63, 'mask_BxS_bk0': mask_BxS_bk0, 'L0_cond_W_ada': _L0_cond_in['W_ada'], 'L0_cond_b_ada': _L0_cond_in['b_ada'], 'L0_cond_Wq': _L0_cond_in['Wq'], 'L0_cond_bq': _L0_cond_in['bq'], 'L0_cond_Wk': _L0_cond_in['Wk'], 'L0_cond_bk': _L0_cond_in['bk'], 'L0_cond_Wv': _L0_cond_in['Wv'], 'L0_cond_bv': _L0_cond_in['bv'], 'L0_cond_Wo': _L0_cond_in['Wo'], 'L0_cond_bo': _L0_cond_in['bo'], 'L0_cond_W1': _L0_cond_in['W1'], 'L0_cond_b1': _L0_cond_in['b1'], 'L0_cond_W2': _L0_cond_in['W2'], 'L0_cond_b2': _L0_cond_in['b2'], 'L1_cond_qkv_w': _L1_cond_in['qkv_w'], 'L1_cond_qkv_b': _L1_cond_in['qkv_b'], 'L1_cond_proj_w': _L1_cond_in['proj_w'], 'L1_cond_proj_b': _L1_cond_in['proj_b'], 'L1_cond_fc1_w': _L1_cond_in['fc1_w'], 'L1_cond_fc1_b': _L1_cond_in['fc1_b'], 'L1_cond_fc2_w': _L1_cond_in['fc2_w'], 'L1_cond_fc2_b': _L1_cond_in['fc2_b'], 'L1_cond_ada_w': _L1_cond_in['ada_w'], 'L1_cond_ada_b': _L1_cond_in['ada_b'], 'L2_cond_w_scale': _L2_cond_in['w_scale'], 'L2_cond_w_offset': _L2_cond_in['w_offset'], 'L2_cond_wq': _L2_cond_in['wq'], 'L2_cond_wk': _L2_cond_in['wk'], 'L2_cond_wv': _L2_cond_in['wv'], 'L2_cond_wo': _L2_cond_in['wo'], 'L2_cond_mlp_ln_scale': _L2_cond_in['mlp_ln_scale'], 'L2_cond_w1': _L2_cond_in['w1'], 'L2_cond_w2': _L2_cond_in['w2'], 'L3_cond_ada_w': _L3_cond_in['ada_w'], 'L3_cond_ada_b': _L3_cond_in['ada_b'], 'L3_cond_ssm_w1': _L3_cond_in['ssm_w1'], 'L3_cond_ssm_b1': _L3_cond_in['ssm_b1'], 'L3_cond_ssm_w2': _L3_cond_in['ssm_w2'], 'L3_cond_ssm_b2': _L3_cond_in['ssm_b2'], 'L3_cond_bwd_w1': _L3_cond_in['bwd_w1'], 'L3_cond_bwd_b1': _L3_cond_in['bwd_b1'], 'L3_cond_bwd_w2': _L3_cond_in['bwd_w2'], 'L3_cond_bwd_b2': _L3_cond_in['bwd_b2'], 'L3_cond_ffada_w': _L3_cond_in['ffada_w'], 'L3_cond_ffada_b': _L3_cond_in['ffada_b'], 'L3_cond_ff_w1': _L3_cond_in['ff_w1'], 'L3_cond_ff_b1': _L3_cond_in['ff_b1'], 'L3_cond_ff_w2': _L3_cond_in['ff_w2'], 'L3_cond_ff_b2': _L3_cond_in['ff_b2']}

def reference(x, cond_1024, itok_BxSx2_0_63, mask_BxS_bk0, L0_cond_W_ada, L0_cond_b_ada, L0_cond_Wq, L0_cond_bq, L0_cond_Wk, L0_cond_bk, L0_cond_Wv, L0_cond_bv, L0_cond_Wo, L0_cond_bo, L0_cond_W1, L0_cond_b1, L0_cond_W2, L0_cond_b2, L1_cond_qkv_w, L1_cond_qkv_b, L1_cond_proj_w, L1_cond_proj_b, L1_cond_fc1_w, L1_cond_fc1_b, L1_cond_fc2_w, L1_cond_fc2_b, L1_cond_ada_w, L1_cond_ada_b, L2_cond_w_scale, L2_cond_w_offset, L2_cond_wq, L2_cond_wk, L2_cond_wv, L2_cond_wo, L2_cond_mlp_ln_scale, L2_cond_w1, L2_cond_w2, L3_cond_ada_w, L3_cond_ada_b, L3_cond_ssm_w1, L3_cond_ssm_b1, L3_cond_ssm_w2, L3_cond_ssm_b2, L3_cond_bwd_w1, L3_cond_bwd_b1, L3_cond_bwd_w2, L3_cond_bwd_b2, L3_cond_ffada_w, L3_cond_ffada_b, L3_cond_ff_w1, L3_cond_ff_b1, L3_cond_ff_w2, L3_cond_ff_b2):
    import jax
    import jax.numpy as jnp

    def _L0_cond_ref(x, c, W_ada, b_ada, Wq, bq, Wk, bk, Wv, bv, Wo, bo, W1, b1, W2, b2):
        import jax, jax.numpy as jnp
        import numpy as np
        D_MODEL = 128
        NHEAD = 16
        HEAD_DIM = D_MODEL // NHEAD
        D_FF = 512
        EPS = 1e-05

        def _layernorm(x):
            mu = jnp.mean(x, axis=-1, keepdims=True)
            var = jnp.var(x, axis=-1, keepdims=True)
            return (x - mu) * jax.lax.rsqrt(var + EPS)
        B, N, _ = x.shape
        ada = (c @ W_ada + b_ada)[:, None, :]
        shift1, scale1, gate1, shift2, scale2, gate2 = jnp.split(ada, 6, axis=-1)
        h = _layernorm(x) * (1.0 + scale1) + shift1
        Q = (h @ Wq + bq).reshape(B, N, NHEAD, HEAD_DIM)
        K = (h @ Wk + bk).reshape(B, N, NHEAD, HEAD_DIM)
        V = (h @ Wv + bv).reshape(B, N, NHEAD, HEAD_DIM)
        scores = jnp.einsum('bqhd,bkhd->bhqk', Q, K) / np.sqrt(HEAD_DIM).astype(np.float32)
        attn = jax.nn.softmax(scores, axis=-1)
        attn_out = jnp.einsum('bhqk,bkhd->bqhd', attn, V).reshape(B, N, D_MODEL)
        attn_out = attn_out @ Wo + bo
        x = x + gate1 * attn_out
        h = _layernorm(x) * (1.0 + scale2) + shift2
        ff = jax.nn.gelu(h @ W1 + b1, approximate=False) @ W2 + b2
        return x + gate2 * ff

    def _L1_cond_ref(x, c, positions, qkv_w, qkv_b, proj_w, proj_b, fc1_w, fc1_b, fc2_w, fc2_b, ada_w, ada_b):
        import jax, jax.numpy as jnp
        import numpy as np
        EPS = 1e-06
        ROPE_BASE = 100.0

        def layernorm(x):
            mu = jnp.mean(x, axis=-1, keepdims=True)
            var = jnp.var(x, axis=-1, keepdims=True)
            return (x - mu) / jnp.sqrt(var + EPS)

        def modulate(x, shift, scale):
            return x * (1.0 + scale[:, None, :]) + shift[:, None, :]

        def rope1d(t, pos):
            d = t.shape[-1]
            inv_freq = 1.0 / ROPE_BASE ** (jnp.arange(0, d, 2, dtype=jnp.float32) / d)
            ang = pos[:, None, :, None] * inv_freq
            ang = jnp.concatenate([ang, ang], axis=-1)
            cos, sin = (jnp.cos(ang), jnp.sin(ang))
            t1, t2 = (t[..., :d // 2], t[..., d // 2:])
            rot = jnp.concatenate([-t2, t1], axis=-1)
            return t * cos + rot * sin

        def rope2d(t, positions):
            hd = t.shape[-1]
            pos = positions.astype(jnp.float32)
            ty = rope1d(t[..., :hd // 2], pos[..., 0])
            tx = rope1d(t[..., hd // 2:], pos[..., 1])
            return jnp.concatenate([ty, tx], axis=-1)
        B, N, D = x.shape
        H = 16
        hd = D // H
        scale = hd ** (-0.5)
        m = jax.nn.silu(c) @ ada_w + ada_b
        shift_msa, scale_msa, gate_msa, shift_mlp, scale_mlp, gate_mlp = jnp.split(m, 6, axis=1)
        h = modulate(layernorm(x), shift_msa, scale_msa)
        qkv = (h @ qkv_w + qkv_b).reshape(B, N, 3, H, hd).transpose(2, 0, 3, 1, 4)
        q, k, v = (qkv[0], qkv[1], qkv[2])
        q = rope2d(q, positions)
        k = rope2d(k, positions)
        attn = jax.nn.softmax(jnp.einsum('bhnd,bhmd->bhnm', q, k) * scale, axis=-1)
        o = jnp.einsum('bhnm,bhmd->bhnd', attn, v).transpose(0, 2, 1, 3).reshape(B, N, D)
        o = o @ proj_w + proj_b
        x = x + gate_msa[:, None, :] * o
        h = modulate(layernorm(x), shift_mlp, scale_mlp)
        h = jax.nn.gelu(h @ fc1_w + fc1_b, approximate=True) @ fc2_w + fc2_b
        x = x + gate_mlp[:, None, :] * h
        return x

    def _L2_cond_ref(x, t_emb, w_scale, w_offset, wq, wk, wv, wo, mlp_ln_scale, w1, w2):
        import jax, jax.numpy as jnp
        import numpy as np
        B, L, D, NH, MLP = (4, 256, 128, 16, 512)
        KD = D // NH
        EPS = 1e-05

        def layer_norm(x, scale=None):
            mu = jnp.mean(x, axis=-1, keepdims=True)
            var = jnp.var(x, axis=-1, keepdims=True)
            y = (x - mu) * jax.lax.rsqrt(var + EPS)
            return y * scale if scale is not None else y

        def rotary_pos_emb(x):
            dim, seq = (x.shape[-1], x.shape[-2])
            inv_freqs = 10000.0 ** (-jnp.arange(0, dim, 2, dtype=jnp.float32) / dim)
            grid = jnp.arange(seq, dtype=jnp.float32)[:, None] * inv_freqs[None, :]
            sin = jnp.repeat(jnp.sin(grid), 2, axis=-1)
            cos = jnp.repeat(jnp.cos(grid), 2, axis=-1)
            x1, x2 = (x[..., ::2], x[..., 1::2])
            xs = jnp.stack([-x2, x1], axis=-1).reshape(x.shape)
            return x * cos + xs * sin
        b, l, d = x.shape
        scale = t_emb @ w_scale
        offset = t_emb @ w_offset
        h = layer_norm(x) * scale + offset
        q = h @ wq / jnp.sqrt(jnp.asarray(d, h.dtype))
        q = q.reshape(b, l, NH, KD).transpose(0, 2, 1, 3)
        k = (h @ wk).reshape(b, l, NH, KD).transpose(0, 2, 1, 3)
        v = (h @ wv).reshape(b, l, NH, KD).transpose(0, 2, 1, 3)
        q = rotary_pos_emb(q)
        k = rotary_pos_emb(k)
        logits = jnp.einsum('bhik,bhjk->bhij', q, k)
        a = jax.nn.softmax(logits, axis=-1)
        y = jnp.einsum('bhij,bhjv->bhiv', a, v)
        y = y.transpose(0, 2, 1, 3).reshape(b, l, d)
        x = x + y @ wo
        h2 = layer_norm(x, mlp_ln_scale)
        h2 = jax.nn.gelu(h2 @ w1) @ w2
        return x + h2

    def _L3_cond_ref(x, t, mask, ada_w, ada_b, ssm_w1, ssm_b1, ssm_w2, ssm_b2, bwd_w1, bwd_b1, bwd_w2, bwd_b2, ffada_w, ffada_b, ff_w1, ff_b1, ff_w2, ff_b2):
        import jax, jax.numpy as jnp
        import numpy as np
        B, L, D = (8, 256, 128)
        FF_MULT = 2
        EPS = 1e-06

        def _layernorm(x):
            mu = jnp.mean(x, axis=-1, keepdims=True)
            var = jnp.mean(jnp.square(x - mu), axis=-1, keepdims=True)
            return (x - mu) / jnp.sqrt(var + EPS)

        def _ssm_fallback(u, w1, b1, w2, b2):
            h = jax.nn.gelu(u @ w1 + b1, approximate=False)
            return h @ w2 + b2
        m = mask[:, :, None]
        emb = jax.nn.silu(t) @ ada_w + ada_b
        shift, scale, gate_msa = jnp.split(emb, 3, axis=1)
        norm = _layernorm(x) * (1.0 + scale[:, None]) + shift[:, None]
        norm = jnp.where(m, norm, 0.0)
        fwd = _ssm_fallback(norm, ssm_w1, ssm_b1, ssm_w2, ssm_b2)
        bwd = jnp.flip(_ssm_fallback(jnp.flip(norm, axis=1), bwd_w1, bwd_b1, bwd_w2, bwd_b2), axis=1)
        ssm_out = jnp.where(m, fwd + bwd, 0.0)
        x = x + gate_msa[:, None] * ssm_out
        ff_ada = jax.nn.silu(t) @ ffada_w + ffada_b
        shift_mlp, scale_mlp, gate_mlp = jnp.split(ff_ada, 3, axis=1)
        ff_norm = _layernorm(x) * (1.0 + scale_mlp[:, None]) + shift_mlp[:, None]
        h = jax.nn.gelu(ff_norm @ ff_w1 + ff_b1, approximate=True)
        ff_out = h @ ff_w2 + ff_b2
        return x + gate_mlp[:, None] * ff_out
    x = _L0_cond_ref(x, cond_1024, L0_cond_W_ada, L0_cond_b_ada, L0_cond_Wq, L0_cond_bq, L0_cond_Wk, L0_cond_bk, L0_cond_Wv, L0_cond_bv, L0_cond_Wo, L0_cond_bo, L0_cond_W1, L0_cond_b1, L0_cond_W2, L0_cond_b2)
    x = _L1_cond_ref(x, cond_1024, itok_BxSx2_0_63, L1_cond_qkv_w, L1_cond_qkv_b, L1_cond_proj_w, L1_cond_proj_b, L1_cond_fc1_w, L1_cond_fc1_b, L1_cond_fc2_w, L1_cond_fc2_b, L1_cond_ada_w, L1_cond_ada_b)
    x = _L2_cond_ref(x, cond_1024[:, None, :], L2_cond_w_scale, L2_cond_w_offset, L2_cond_wq, L2_cond_wk, L2_cond_wv, L2_cond_wo, L2_cond_mlp_ln_scale, L2_cond_w1, L2_cond_w2)
    x = _L3_cond_ref(x, cond_1024, mask_BxS_bk0, L3_cond_ada_w, L3_cond_ada_b, L3_cond_ssm_w1, L3_cond_ssm_b1, L3_cond_ssm_w2, L3_cond_ssm_b2, L3_cond_bwd_w1, L3_cond_bwd_b1, L3_cond_bwd_w2, L3_cond_bwd_b2, L3_cond_ffada_w, L3_cond_ffada_b, L3_cond_ff_w1, L3_cond_ff_b1, L3_cond_ff_w2, L3_cond_ff_b2)
    return x

_drawn_inputs = setup_inputs


def setup_inputs(seed=0):
    import zlib

    import numpy as np

    out = dict(_drawn_inputs(seed))
    spreads = {'L0_cond_b_ada': (0.0, 0.58),
     'L0_cond_bq': (0.0, 0.8),
     'L0_cond_bk': (0.0, 2.0),
     'L0_cond_bv': (0.0, 0.8),
     'L0_cond_bo': (0.0, 0.325),
     'L0_cond_b1': (0.0, 0.8),
     'L0_cond_b2': (0.0, 0.329),
     'L1_cond_qkv_b': (0.0, 0.509),
     'L1_cond_proj_b': (0.0, 0.57),
     'L1_cond_fc1_b': (0.0, 0.85),
     'L1_cond_fc2_b': (0.0, 0.483),
     'L1_cond_ada_b': (0.0, 0.1),
     'L2_cond_mlp_ln_scale': (1.0, 0.2),
     'L3_cond_ada_b': (0.0, 0.8),
     'L3_cond_ssm_b1': (0.0, 0.8),
     'L3_cond_ssm_b2': (0.0, 0.8),
     'L3_cond_bwd_b1': (0.0, 0.8),
     'L3_cond_bwd_b2': (0.0, 0.8),
     'L3_cond_ffada_b': (0.0, 0.8),
     'L3_cond_ff_b1': (0.0, 0.8),
     'L3_cond_ff_b2': (0.0, 0.8)}
    factors = {'L0_cond_Wq': 8.0,
     'L0_cond_Wk': 8.0,
     'L0_cond_Wv': 8.0,
     'L0_cond_Wo': 6.514,
     'L0_cond_W1': 6.183,
     'L0_cond_W2': 5.203,
     'L2_cond_wq': 2.947,
     'L2_cond_wk': 3.147,
     'L3_cond_ada_w': 8.0,
     'L3_cond_ssm_w1': 8.0,
     'L3_cond_ssm_w2': 8.0,
     'L3_cond_bwd_w1': 8.0,
     'L3_cond_bwd_w2': 8.0,
     'L3_cond_ffada_w': 8.0,
     'L3_cond_ff_w1': 8.0,
     'L3_cond_ff_w2': 8.0}
    for name, (base, spread) in spreads.items():
        noise = np.random.default_rng([zlib.crc32(name.encode()), seed]).standard_normal(out[name].shape)
        drawn = base * np.exp(spread * noise) if base else spread * noise
        out[name] = jnp.asarray(drawn.astype(out[name].dtype))
    for name, factor in factors.items():
        out[name] = (out[name] * factor).astype(out[name].dtype)
    return out
```

```python
from contextlib import ExitStack

import numpy as np

import concourse.bass as bass
from concourse import mybir

F32 = mybir.dt.float32
BF16 = mybir.dt.bfloat16
I32 = mybir.dt.int32
U8 = mybir.dt.uint8
ALU = mybir.AluOpType
ACT = mybir.ActivationFunctionType
AX_X = mybir.AxisListType.X

P = 128
NB, S, D, H, HD, FF = 2, 512, 128, 16, 8, 512
T = S // P
LAYERS = 3
CHAINS = LAYERS * NB
GROUPS = H // 4
SCORE_SCALE = [HD ** -0.5, HD ** -0.5, D ** -0.5]
EPS = [1e-5, 1e-6, 1e-5, 1e-6]
PARTS_Q = [0, 0, 0, 1, 1, 2]
PARTS_K = [0, 1, 2, 0, 1, 0]
MAX_ROW = 96
RING_P = 12

MOD = 14
V_BIAS, V_ONE, V_BQ, V_BK, V_BV, V_B1, V_LN2, V_SSM1, V_FF1, V_ZERO, V_N = 0, 14, [28, 31, 50], [29, 32, 50], [30, 33, 50], [34, 38, None], 42, 43, 45, 50, 51
W_Q, W_K, W_V, W_O, W_1, W_2 = 0, 128, 256, 384, 512, 1024
STRIDE = 17
LAG_B = 6
LAG_V = 1


def chain_of_job_layers(k):
    return k // NB, k % NB


def dense_items(k):
    layer = k // NB
    items = []
    if layer > 0:
        items += [("OT", 2), ("WO", 1), ("XH", 1), ("TR", 2), ("W1", 1), ("W2", 1)]
    if layer == LAYERS:
        items += [("XH", 1), ("TR", 2), ("MK", 1), ("W1S", 1), ("W2S", 1), ("XH", 1), ("TR", 2), ("W1F", 1), ("W2F", 1)]
        return items
    if layer == 0:
        items += [("ST", 1)]
    items += [("XH", 1), ("TR", 2), ("K", 1), ("Q", 1), ("V", 1)]
    if layer > 0:
        items += [("RK", 1), ("RQ", 1)]
    items += [("SQ", 1), ("DQK", 1)]
    return items


PLACES = (0, 2, 3)


def make_plan():
    last = STRIDE * (CHAINS - 1) + LAG_B + H + LAG_V + 1
    plan = [[[] for _ in PLACES] for _ in range(last + 60)]

    def put(at, item):
        plan[at // 3][at % 3].append(item)
        return at

    def put_job(k, at, items=None):
        for name, gap in items or dense_items(k):
            put(at, (name, k))
            at += gap
        return at

    plan[0][0] = [(name, 0) for name, _ in dense_items(0)] + [("ADA1", 0), ("GATE", 0)]
    plan[0][0].insert(1, ("ADA0", 0))
    end = put_job(1, 3)
    put(3 * 5, ("XG0", 0))
    at = 3 * 10
    for b in range(NB):
        put(at, ("ANG", b)); at += 1
        for f in range(2):
            put(at, ("RED", 2 * b + f)); at += 3
    put(at + 3, ("SIN", 0))
    for q in range(CHAINS):
        for g in range(GROUPS):
            put(3 * (first_slot(q) + LAG_B + 4 * g + 3 + LAG_V) + 2, ("OG", GROUPS * q + g))
        k = q + NB
        start = 3 * (first_slot(q) + LAG_B + H + LAG_V) + 1
        end = put_job(k, max(start, end))
    used = max(s for s, sl in enumerate(plan) if any(sl))
    return plan[:used + 1]


def first_slot(q):
    return 1 + STRIDE * q


PLAN = make_plan()
SLOTS = len(PLAN)


def maxima_of(s):
    for q in range(CHAINS):
        if 0 <= s - first_slot(q) < H:
            return q, s - first_slot(q)
    return None


def exps_of(s):
    for q in range(CHAINS):
        n = s - first_slot(q) - LAG_B
        if 0 <= n < H:
            return GROUPS * q + n // 4, n % 4
    return None


def max_rows_of(s):
    for q in range(CHAINS):
        n = s - first_slot(q)
        if n in (4, 8, 12, 16):
            return GROUPS * q + n // 4 - 1
    return None


def uses_of_dense_bank(name):
    if name in ("ADA0", "ADA1", "OG", "OT", "WO", "TR", "W2", "W2S", "W2F", "K", "Q", "V", "RK", "RQ", "ANG"):
        return 1
    return {"W1": 4, "W1S": 2, "W1F": 2}.get(name, 0)


def number_uses():
    dense, tiles, stats, xg, count = {}, {}, {}, {}, {}
    nd = nt = 0
    for s in range(SLOTS):
        for i in range(4):
            if maxima_of(s):
                tiles[("max", s, i)] = nt
                nt += 1
            if i == 2 and max_rows_of(s) is not None:
                tiles[("rows", s)] = nt
                nt += 1
            if i in PLACES:
                for item in PLAN[s][PLACES.index(i)]:
                    dense[item + (count.get(("n",) + item, 0),)] = nd
                    nd += uses_of_dense_bank(item[0])
                    count[("n",) + item] = count.get(("n",) + item, 0) + 1
    return dense, tiles


DENSE_USE, TILE_USE = number_uses()


def walk():
    seen = {}
    for s in range(SLOTS):
        for i in range(4):
            items = []
            if i in PLACES:
                for item in PLAN[s][PLACES.index(i)]:
                    n = seen.get(item, 0)
                    seen[item] = n + 1
                    items.append((item[0], item[1], n))
            yield s, i, items


def norm_order():
    norm_no, n = {}, 0
    gated_no, g = {}, 0
    for _, _, items in walk():
        for name, k, c in items:
            if name == "XH":
                norm_no[(k, c)] = n
                n += 1
            if name == "XG0":
                gated_no[("WO", 2)], gated_no[("WO", 3)] = g, g + 1
                g += 2
            layer = k // NB
            nxt = {"WO": ("W2", k) if layer in (1, 2) else None,
                   "W2": ("WO", k + 2) if layer == 1 else ("W2S", k) if layer == 3 else None,
                   "W2S": ("W2F", k)}.get(name)
            if nxt:
                gated_no[nxt] = g
                g += 1
    return norm_no, gated_no


NORM_NO, GATED_NO = norm_order()
GATE_OF = {("WO", 1): (0, 0), ("W2", 1): (0, 1), ("WO", 2): (1, 0), ("W2", 2): (1, 1), ("W2S", 3): (2, 0), ("W2F", 3): (2, 1)}


def next_gated(name, k):
    layer = k // NB
    if name == "WO" and layer in (1, 2):
        return "W2", k
    if name == "W2" and layer == 1:
        return "WO", k + 2
    if name == "W2" and layer == 3:
        return "W2S", k
    if name == "W2S":
        return "W2F", k
    return None


def build(nc, ins, y):
    ctx = ExitStack()
    with ctx:
        def sb(name, shape, dt=F32):
            return ctx.enter_context(nc.sbuf_tensor(name, shape, dt))

        def sem(name):
            return ctx.enter_context(nc.semaphore(name))

        x = sb("x", [P, NB, T, D])
        xg = sb("xg", [P, NB, T, D])
        q_stack = sb("q_stack", [P, NB, H, S], BF16)
        k_stack = sb("k_stack", [P, NB, H, S], BF16)
        v_ones = sb("v_ones", [P, NB, T, H, 32])
        probs = sb("probs", [P, RING_P, S])
        w = [sb(f"w{n}", [P, 1536 if n < LAYERS else 1024]) for n in range(LAYERS + 1)]
        vec = sb("vec", [P, V_N])
        modv = sb("modv", [P, MOD, NB])
        gate = sb("gate", [P, 3, 2, NB, D])
        gate_b = sb("gate_b", [P, 3, 2, NB, D])
        ident = sb("ident", [P, P])
        ident_bf = sb("ident_bf", [P, P], BF16)
        turn = sb("turn", [P, 2, P])
        freq = sb("freq", [2, P])
        pos_i = sb("pos_i", [2, NB, S], I32)
        pos_f = sb("pos_f", [2, NB, S])
        rot1 = sb("rot1", [P, NB, 2, S])
        rot2 = sb("rot2", [P, 2, S])
        mask_words = sb("mask_words", [P, NB, S // 4], I32)
        mask_row = mask_words[:, :, :].bitcast(U8)
        mask_col_words = sb("mask_col_words", [P, NB * T // 4], I32)
        mask_u8 = mask_col_words[:, :].bitcast(U8).rearrange("p (b t) -> p b t", b=NB)
        mask_col = sb("mask_col", [P, NB, T])
        cond = sb("cond", [P, NB])
        silu = sb("silu", [P, 4, NB])
        xhat = sb("xhat", [P, 2, T, D])
        hT = sb("hT", [P, 2, S])
        work = sb("work", [P, 6, S])
        hid = work[:, 0:4]
        parts = sb("parts", [P, 2, 3, S], BF16)
        oT_raw = sb("oT_raw", [P, S])
        o_tok = sb("o_tok", [P, T, D])
        oT = sb("oT", [P, S])
        rden = sb("rden", [P, T, 4])
        gated = work[:, 5].rearrange("p (t d) -> p t d", t=T)
        bst = sb("bst", [P, T, 6])
        mv = sb("mv", [P, 2, T, 2])
        rstd = sb("rstd", [P, 2, T])
        half = sb("half", [P, 5])
        mx = sb("mx", [P, 2, T, 4])
        mres = sb("mres", [P, 2, T, 4])
        mparts = sb("mparts", [P, 2, T, 3, 4], BF16)
        mrows = sb("mrows", [12, 2, S], BF16)
        ang, turns = work[:, 2], work[:, 3]
        pflat = probs[:, :, :].rearrange("p a b -> p (a b)")
        ada = pflat[:, 0:2560]
        rows = pflat[:, 2560:2560 + 13 * D]
        cwide = pflat[:, 4608:4608 + 4 * P].rearrange("p (a n) -> p a n", a=4)

        max_ps = ctx.enter_context(nc.psum_tensor("max_ps", [P, 2, S], F32))
        exp_ps = ctx.enter_context(nc.psum_tensor("exp_ps", [P, 3, S], F32))
        pv_ps = ctx.enter_context(nc.psum_tensor("pv_ps", [P, S], F32))
        dense_ps = ctx.enter_context(nc.psum_tensor("dense_ps", [P, 2, S], F32))

        x_in = [sem(f"x{b}_in") for b in range(NB)]
        small_in, ada0_in, ada1_in, rows_in = sem("small_in"), sem("ada0_in"), sem("ada1_in"), sem("rows_in")
        w_in = [sem(f"w{n}_in") for n in range(LAYERS + 1)]
        late_in = sem("late_in")
        stack_zero = [sem(f"stack_zero{b}") for b in range(NB)]
        v_set = [sem(f"v_set{b}") for b in range(NB)]
        zeros_set, ones_set = sem("zeros_set"), sem("ones_set")
        stacked = [sem(f"stacked{b}") for b in range(NB)]
        tile_full, tile_free = sem("tile_full"), sem("tile_free")
        max_split = sem("max_split")
        rows_in_stack = [sem(f"rows_in_stack{n}") for n in range(2)]
        shifted, exp_done, quad_done, quad_out = sem("shifted"), sem("exp_done"), sem("quad_done"), sem("quad_out")
        v_ready, o_ready = sem("v_ready"), sem("o_ready")
        dense_full = sem("dense_full")
        res_read, ang_read = sem("res_read"), sem("ang_read")
        cond_ready, silu_exp, mod_ready = sem("cond_ready"), sem("silu_exp"), sem("mod_ready")
        gates_full, gates_ready, gate_b_ready = sem("gates_full"), sem("gates_ready"), sem("gate_b_ready")
        id_ready, pos_ready, ang_ready, sincos = sem("id_ready"), sem("pos_ready"), sem("ang_ready"), sem("sincos")
        stats_ready, rstd_ready, xhat_ready, h_ready, h_masked = sem("stats_ready"), sem("rstd_ready"), sem("xhat_ready"), sem("h_ready"), sem("h_masked")
        qk_ready, cos_done, roped, split_k, split_q = sem("qk_ready"), sem("cos_done"), sem("roped"), sem("split_k"), sem("split_q")
        oT_ready, hid_ready, xg_ready, y_ready, y_out = sem("oT_ready"), sem("hid_ready"), sem("xg_ready"), sem("y_ready"), sem("y_out")
        dve_step, pool_step = sem("dve_step"), sem("pool_step")

        def use(item):
            return DENSE_USE[item]

        def bank(n):
            return dense_ps[:, n % 2, :]

        def h_item(k, c):
            return NORM_NO[(k, c)]

        MLP = {"W1": (4, 0), "W1S": (2, 1), "W1F": (2, 2)}

        def mlp_weights(name, layer):
            if name in ("W1", "W2"):
                t = w[layer - 1]
                return t[:, W_1:W_1 + FF], t[:, W_2:W_2 + FF]
            t = w[LAYERS]
            return (t[:, 0:256], t[:, 256:512]) if name in ("W1S", "W2S") else (t[:, 512:768], t[:, 768:1024])

        def norm_of(name, k):
            layer = k // NB
            if layer == 0:
                return NORM_NO[(k, 0)]
            if name == "W1":
                return NORM_NO[(k, 0)]
            if name == "W1F":
                return NORM_NO[(k, 2)]
            return NORM_NO[(k, 1)]

        hid_no = {}
        for _, _, items in walk():
            for name, k, c in items:
                if name in MLP:
                    hid_no[(name, k)] = (max(hid_no.values()) if hid_no else 0) + MLP[name][0]

        read_of, residuals = {}, 0
        residual_no = {}
        for _, _, items in walk():
            for name, k, c in items:
                n = DENSE_USE[(name, k, c)]
                if name in ("WO", "W2", "W2S", "W2F"):
                    residuals += 1
                    residual_no[(name, k)] = residuals
                for j in range(uses_of_dense_bank(name)):
                    read_of[n + j] = {
                        "ADA0": (mod_ready, 1), "ADA1": (mod_ready, 2), "V": (v_ready, k + 1),
                        "TR": (h_ready, NORM_NO.get((k, c), 0) + 1), "K": (qk_ready, 2 * k + 1), "Q": (qk_ready, 2 * k + 2),
                        "OT": (oT_ready, k - NB + 1), "OG": (o_ready, k + 1), "ANG": (ang_read, k + 1),
                        "RK": (roped, 2 * (k - NB) + 1), "RQ": (roped, 2 * (k - NB) + 2),
                    }.get(name) or ((hid_ready, hid_no[(name, k)] - MLP[name][0] + j + 1) if name in MLP else (res_read, residuals))

        block = ctx.enter_context(nc.Block())

        @block.sync
        def _(sp):
            sp.dma_start(x[:, 0], ins["x"][0].rearrange("(t p) d -> p t d", p=P)).then_inc(x_in[0], 16)
            sp.dma_start(cond[:, :], ins["cond"]).then_inc(small_in, 16)
            sp.dma_start(vec[:, :], ins["vec"]).then_inc(small_in, 16)
            sp.dma_start(ident[:, :], ins["ident"]).then_inc(small_in, 16)
            sp.dma_start(ada[:, 0:768], ins["ada"][:, 0:768]).then_inc(ada0_in, 16)
            sp.dma_start(w[0][:, 0:512], ins["w0"][:, 0:512]).then_inc(w_in[0], 16)
            sp.dma_start(x[:, 1], ins["x"][1].rearrange("(t p) d -> p t d", p=P)).then_inc(x_in[1], 16)
            sp.dma_start(ada[:, 768:2560], ins["ada"][:, 768:2560]).then_inc(ada1_in, 16)
            sp.dma_start(rows, ins["rows"].to_broadcast([P, 13 * D])).then_inc(rows_in, 16)

            def stack(k, which, target, of_part, split_done):
                layer, b = chain_of_job_layers(k)
                sp.wait_ge(split_done, k + 1)
                for r, part in enumerate(of_part):
                    sp.dma_start(target[8 * r:8 * r + 8, b], parts[:, which, part, :]).then_inc(stacked[b], 16)

            for s, i, items in walk():
                if i == 3 and max_rows_of(s) is not None:
                    G = max_rows_of(s)
                    b = (G // GROUPS) % NB
                    sp.wait_ge(tile_free, TILE_USE[("rows", s)] + 1)
                    for part in range(3):
                        sp.dma_start(q_stack[MAX_ROW + part:MAX_ROW + part + 1, b, 4 * (G % GROUPS):4 * (G % GROUPS) + 4, :],
                                     mrows[4 * part:4 * part + 4, G % 2, :]).then_inc(rows_in_stack[G % 2], 16)
                for name, k, c in items:
                    if name == "DQK":
                        if k < NB:
                            sp.wait_ge(stack_zero[k], 2)
                        stack(k, 0, k_stack, PARTS_K, split_k)
                        stack(k, 1, q_stack, PARTS_Q, split_q)
                        if k == 0:
                            sp.dma_start(w[0][:, 512:1536], ins["w0"][:, 512:1536]).then_inc(w_in[0], 16)
                            sp.dma_start(turn[:, :, :], ins["turn"]).then_inc(late_in, 16)
                            sp.dma_start(freq[:, :], ins["freq"]).then_inc(late_in, 16)
                            sp.dma_start(pos_i[:, :, :], ins["pos"]).then_inc(late_in, 16)
                            sp.dma_start(rot2[:, :, :], ins["rot2"]).then_inc(late_in, 16)
                            for b in range(NB):
                                sp.dma_start(mask_words[:, b, :], ins["mask_row"][b:b + 1, :].to_broadcast([P, S // 4])).then_inc(late_in, 16)
                            sp.dma_start(mask_col_words[:, :], ins["mask_col"]).then_inc(late_in, 16)
                            for n in range(1, LAYERS + 1):
                                sp.dma_start(w[n][:, :], ins[f"w{n}"]).then_inc(w_in[n], 16)
            for b in range(NB):
                sp.wait_ge(y_ready, b + 1)
                sp.dma_start(y[b].rearrange("(t p) d -> p t d", p=P), x[:, b]).then_inc(y_out, 16)
            sp.wait_ge(y_out, 16 * NB)
        LATE = 16 * 7

        @block.tensor
        def _(pe):
            def take(n):
                if n >= 2:
                    pe.wait_ge(*read_of[n - 2])

            def turn_tiles(n, src):
                for t in range(T):
                    mm = pe.transpose(bank(n)[:, t * P:(t + 1) * P], src(t), ident[:, :])
                mm.then_inc(dense_full, 1)

            def token_product(n, lhs, weights):
                for t in range(T):
                    mm = pe.matmul(bank(n)[:, t * D:(t + 1) * D], lhs[:, t * P:(t + 1) * P], weights, start=True, stop=True)
                mm.then_inc(dense_full, 1)

            def dense(item):
                name, k, c = item
                layer, b = chain_of_job_layers(k)
                n = use(item)
                if name == "ADA0":
                    pe.wait_ge(ada0_in, 16)
                    pe.wait_ge(small_in, 48)
                    take(n)
                    for m, col in enumerate((0, 1, 3, 4)):
                        mm = pe.matmul(bank(n)[:, 2 * m:2 * m + 2], ada[:, col * D:(col + 1) * D], cond[:, :], start=True, stop=True)
                    mm.then_inc(dense_full, 1)
                elif name == "ADA1":
                    pe.wait_ge(ada1_in, 16)
                    pe.wait_ge(cond_ready, 2)
                    take(n)
                    cols = [(6, 1), (7, 1), (9, 1), (10, 1), (12, 0), (13, 0), (14, 1), (15, 1), (17, 1), (18, 1)]
                    for m, (col, act) in enumerate(cols):
                        rhs = silu[:, 3, :] if act else cond[:, :]
                        mm = pe.matmul(bank(n)[:, 2 * m:2 * m + 2], ada[:, col * D:(col + 1) * D], rhs, start=True, stop=True)
                    mm.then_inc(dense_full, 1)
                elif name == "GATE":
                    pe.wait_ge(cond_ready, 3)
                    for r, (cols, act) in enumerate((((2, 5), 0), ((8, 11), 1), ((16, 19), 1))):
                        for g, col in enumerate(cols):
                            for bb in range(NB):
                                o = (2 * g + bb) * D
                                mm = pe.matmul(exp_ps[:, r, o:o + D], cwide[:, 2 * act + bb, :], ada[:, col * D:(col + 1) * D], start=True, stop=True)
                    mm.then_inc(gates_full, 1)
                elif name == "TR":
                    i = NORM_NO[(k, c)]
                    pe.wait_ge(xhat_ready, i + 1)
                    take(n)
                    turn_tiles(n, lambda t: xhat[:, i % 2, t, :])
                elif name in ("K", "Q"):
                    i = norm_of(name, k)
                    pe.wait_ge(h_ready, i + 1)
                    pe.wait_ge(w_in[layer], 16)
                    take(n)
                    o = W_K if name == "K" else W_Q
                    pe.matmul(bank(n), w[layer][:, o:o + D], hT[:, i % 2, :], start=True, stop=True).then_inc(dense_full, 1)
                elif name == "V":
                    i = norm_of(name, k)
                    pe.wait_ge(h_ready, i + 1)
                    take(n)
                    token_product(n, hT[:, i % 2, :], w[layer][:, W_V:W_V + D])
                elif name in ("RK", "RQ"):
                    pe.wait_ge(qk_ready, 2 * k + (1 if name == "RK" else 2))
                    if k == NB:
                        pe.wait_ge(late_in, LATE)
                    take(n)
                    pe.matmul(bank(n), turn[:, layer - 1, :], work[:, 0 if name == "RK" else 1, :], start=True, stop=True).then_inc(dense_full, 1)
                elif name == "ANG":
                    pe.wait_ge(pos_ready, 1)
                    take(n)
                    pe.matmul(bank(n), freq[:, :], pos_f[:, k, :], start=True, stop=True).then_inc(dense_full, 1)
                elif name == "OG":
                    pe.wait_ge(quad_out, k + 1)
                    take(n)
                    turn_tiles(n, lambda t: oT_raw[:, t * P:(t + 1) * P])
                elif name == "OT":
                    q = k - NB
                    pe.wait_ge(o_ready, GROUPS * (q + 1))
                    take(n)
                    turn_tiles(n, lambda t: o_tok[:, t, :])
                elif name == "WO":
                    pe.wait_ge(oT_ready, k - NB + 1)
                    take(n)
                    token_product(n, oT, w[layer - 1][:, W_O:W_O + D])
                elif name in MLP:
                    chunks = MLP[name][0]
                    i = norm_of(name, k)
                    if name == "W1S":
                        pe.wait_ge(h_masked, b + 1)
                    else:
                        pe.wait_ge(h_ready, i + 1)
                    if name == "W1":
                        pe.wait_ge(w_in[layer - 1], 32 if layer == 1 else 16)
                    else:
                        pe.wait_ge(w_in[LAYERS], 16)
                    w1, _ = mlp_weights(name, layer)
                    for j in range(chunks):
                        take(n + j)
                        pe.matmul(bank(n + j), w1[:, j * P:(j + 1) * P], hT[:, i % 2, :], start=True, stop=True).then_inc(dense_full, 1)
                elif name in ("W2", "W2S", "W2F"):
                    first = name.replace("2", "1")
                    chunks = MLP[first][0]
                    _, w2 = mlp_weights(name, layer)
                    pe.wait_ge(hid_ready, hid_no[(first, k)])
                    take(n)
                    for t in range(T):
                        for j in range(chunks):
                            mm = pe.matmul(bank(n)[:, t * D:(t + 1) * D], hid[:, j, t * P:(t + 1) * P], w2[:, j * D:(j + 1) * D],
                                           start=(j == 0), stop=(j == chunks - 1))
                    mm.then_inc(dense_full, 1)

            for s, i, items in walk():
                if exps_of(s):
                    G, kt = exps_of(s)
                    q, g = G // GROUPS, G % GROUPS
                    b, h, n = q % NB, 4 * g + i, 16 * G + 4 * kt + i
                    if kt == 0 and i == 0:
                        pe.wait_ge(rows_in_stack[G % 2], 48 * (G // 2 + 1))
                        if G == 0:
                            pe.wait_ge(ones_set, 2)
                            pe.wait_ge(gates_ready, 1)
                    if n >= 3:
                        pe.wait_ge(exp_done, n - 2)
                    pe.matmul(exp_ps[:, n % 3, :], k_stack[:, b, h, kt * P:(kt + 1) * P], q_stack[:, b, h, :],
                              start=True, stop=True).then_inc(shifted, 1)
                if maxima_of(s):
                    q, h = maxima_of(s)
                    b, n = q % NB, TILE_USE[("max", s, i)]
                    if h == 0 and i == 0:
                        pe.wait_ge(stacked[b], 192 * (q // NB + 1))
                    if n >= 2:
                        pe.wait_ge(tile_free, n - 1)
                    pe.matmul(max_ps[:, n % 2, :], q_stack[0:MAX_ROW, b, h, i * P:(i + 1) * P], k_stack[0:MAX_ROW, b, h, :],
                              start=True, stop=True).then_inc(tile_full, 1)
                if i == 1 and exps_of(s - LAG_V):
                    G, kt = exps_of(s - LAG_V)
                    q, g = G // GROUPS, G % GROUPS
                    b = q % NB
                    pe.wait_ge(exp_done, 16 * G + 4 * kt + 4)
                    if kt == 0:
                        pe.wait_ge(v_ready, q + 1)
                        if G > 0:
                            pe.wait_ge(quad_out, G)
                    for j in range(4):
                        n = 16 * G + 4 * kt + j
                        mm = pe.matmul(pv_ps[32 * j:32 * j + 32, :], v_ones[:, b, kt, 4 * g + j, :], probs[:, n % RING_P, :],
                                       start=(kt == 0), stop=(kt == T - 1))
                    mm.then_inc(quad_done, 1)
                if i == 2 and max_rows_of(s) is not None:
                    G = max_rows_of(s)
                    n = TILE_USE[("rows", s)]
                    pe.wait_ge(max_split, G + 1)
                    pe.wait_ge(tile_free, n - 1)
                    out = max_ps[:, n % 2, :].bitcast(BF16)
                    for t in range(T):
                        mm = pe.transpose(out[0:12, t * P:(t + 1) * P], mparts[:, G % 2, t].rearrange("p a b -> p (a b)"), ident_bf[:, :])
                    mm.then_inc(tile_full, 1)
                for item in items:
                    dense(item)

        @block.scalar
        def _(act):
            def dense(item):
                name, k, c = item
                layer, b = chain_of_job_layers(k)
                n = use(item)
                if name == "ADA0":
                    act.wait_ge(small_in, 48)
                    act.activation(silu[:, 0, :], cond[:, :], ACT.Exp, scale=-1.0).then_inc(silu_exp, 1)
                elif name == "TR":
                    i = NORM_NO[(k, c)]
                    if layer == 0:
                        act.wait_ge(mod_ready, 1)
                        sh, sc = modv[:, 0, b:b + 1], modv[:, 1, b:b + 1]
                    else:
                        act.wait_ge(mod_ready, 2)
                        cols = {(1, 0): 2, (1, 1): 4, (2, 0): 6, (2, 1): 8, (3, 1): 10, (3, 2): 12}.get((layer, c))
                        if cols is None:
                            sh, sc = vec[:, V_ZERO:V_ZERO + 1], vec[:, V_LN2:V_LN2 + 1]
                        else:
                            sh, sc = modv[:, cols, b:b + 1], modv[:, cols + 1, b:b + 1]
                    act.wait_ge(dense_full, n + 1)
                    act.activation(hT[:, i % 2, :], bank(n), ACT.Identity, bias=sh, scale=sc).then_inc(h_ready, 1)
                elif name in ("K", "Q"):
                    col = (V_BK if name == "K" else V_BQ)[layer]
                    act.wait_ge(dense_full, n + 1)
                    act.activation(work[:, 0 if name == "K" else 1, :], bank(n), ACT.Identity, bias=vec[:, col:col + 1]).then_inc(qk_ready, 1)
                elif name == "OT":
                    col = V_BV[layer - 1]
                    act.wait_ge(dense_full, n + 1)
                    act.activation(oT[:, :], bank(n), ACT.Identity, bias=vec[:, col:col + 1]).then_inc(oT_ready, 1)
                elif name in MLP:
                    chunks = MLP[name][0]
                    if name == "W1":
                        col = V_B1[layer - 1]
                    else:
                        col = V_SSM1 if name == "W1S" else V_FF1
                    f = ACT.Gelu if name == "W1S" or (name == "W1" and layer == 1) else ACT.Gelu_apprx_tanh
                    for j in range(chunks):
                        bias = vec[:, V_ZERO:V_ZERO + 1] if col is None else vec[:, col + j:col + j + 1]
                        act.wait_ge(dense_full, n + j + 1)
                        act.activation(hid[:, j, :], bank(n + j), f, bias=bias).then_inc(hid_ready, 1)
                elif name == "SIN":
                    act.wait_ge(ang_ready, 4)
                    act.activation(rot1[:, :, :, :], rot1[:, :, :, :], ACT.Sin).then_inc(sincos, 1)

            act.wait_ge(zeros_set, 1)
            for t in (k_stack, q_stack):
                act.activation(t[:, 1].rearrange("p h s -> p (h s)").bitcast(F32), half[:, 4:5].to_broadcast([P, H * S // 2]), ACT.Copy).then_inc(stack_zero[1], 1)
            act.activation(v_ones[:, 1].rearrange("p t h e -> p (t h e)"), half[:, 4:5].to_broadcast([P, T * H * 32]), ACT.Copy).then_inc(v_set[1], 1)

            for s, i, items in walk():
                if exps_of(s):
                    G, kt = exps_of(s)
                    n = 16 * G + 4 * kt + i
                    act.wait_ge(shifted, n + 1)
                    if n == 0:
                        act.wait_ge(gate_b_ready, 1)
                    if n >= RING_P:
                        act.wait_ge(quad_done, (n - RING_P) // 4 + 1)
                    act.activation(probs[:, n % RING_P, :], exp_ps[:, n % 3, :], ACT.Exp,
                                   scale=SCORE_SCALE[G // GROUPS // NB]).then_inc(exp_done, 1)
                if i == 2 and exps_of(s - LAG_V) and exps_of(s - LAG_V)[1] == T - 1:
                    G = exps_of(s - LAG_V)[0]
                    act.wait_ge(quad_done, 4 * G + 4)
                    if G > 0:
                        act.wait_ge(dense_full, use(("OG", G - 1, 0)) + 1)
                    act.activation(oT_raw[:, :], pv_ps[:, :], ACT.Copy).then_inc(quad_out, 1)
                for item in items:
                    dense(item)

        @block.vector
        def _(dve):
            steps = [0]

            def settle(ins):
                steps[0] += 1
                ins.then_inc(dve_step, 1)
                dve.wait_ge(dve_step, steps[0])

            def statistics(b, i):
                for t in range(T):
                    ins = dve.bn_stats(bst[:, t, :], x[:, b, t, :])
                settle(ins)
                for t in range(T):
                    ins = dve.bn_aggr(mv[:, i % 2, t, :], bst[:, t, :])
                ins.then_inc(stats_ready, 1)

            def split(src, res, which, done_sem):
                settle(dve.tensor_copy(parts[:, which, 0, :], src))
                settle(dve.tensor_tensor(res, src, parts[:, which, 0, :], ALU.subtract))
                settle(dve.tensor_copy(parts[:, which, 1, :], res))
                dve.tensor_tensor(parts[:, which, 2, :], res, parts[:, which, 1, :], ALU.subtract).then_inc(done_sem, 1)

            def dense(item):
                name, k, c = item
                layer, b = chain_of_job_layers(k)
                n = use(item)
                if name == "ADA0":
                    dve.wait_ge(dense_full, n + 1)
                    settle(dve.tensor_tensor(modv[:, 0:4, :], bank(n)[:, 0:8].rearrange("p (m b) -> p m b", b=NB),
                                             vec[:, V_BIAS:V_BIAS + 4].unsqueeze(2).to_broadcast([P, 4, NB]), ALU.add))
                    dve.tensor_tensor(modv[:, 0:4, :], modv[:, 0:4, :],
                                      vec[:, V_ONE:V_ONE + 4].unsqueeze(2).to_broadcast([P, 4, NB]), ALU.add).then_inc(mod_ready, 1)
                    dve.wait_ge(silu_exp, 1)
                    settle(dve.tensor_scalar(silu[:, 1, :], silu[:, 0, :], 1.0, None, ALU.add))
                    settle(dve.reciprocal(silu[:, 2, :], silu[:, 1, :]))
                    dve.tensor_tensor(silu[:, 3, :], silu[:, 2, :], cond[:, :], ALU.mult).then_inc(cond_ready, 1)
                    dve.tensor_copy(ident_bf[:, :], ident[:, :]).then_inc(cond_ready, 1)
                    dve.wait_ge(cond_ready, 2)
                    dve.tensor_copy(cwide[:, 0:2, :], cond[:, :].unsqueeze(2).to_broadcast([P, NB, P]))
                    dve.tensor_copy(cwide[:, 2:4, :], silu[:, 3, :].unsqueeze(2).to_broadcast([P, NB, P])).then_inc(cond_ready, 1)
                elif name == "ADA1":
                    dve.wait_ge(dense_full, n + 1)
                    settle(dve.tensor_tensor(modv[:, 4:14, :], bank(n)[:, 0:20].rearrange("p (m b) -> p m b", b=NB),
                                             vec[:, V_BIAS + 4:V_BIAS + 14].unsqueeze(2).to_broadcast([P, 10, NB]), ALU.add))
                    dve.tensor_tensor(modv[:, 4:14, :], modv[:, 4:14, :],
                                      vec[:, V_ONE + 4:V_ONE + 14].unsqueeze(2).to_broadcast([P, 10, NB]), ALU.add).then_inc(mod_ready, 1)
                elif name == "GATE":
                    dve.wait_ge(gates_full, 1)
                    dve.wait_ge(rows_in, 16)
                    for r in range(3):
                        ins = dve.tensor_tensor(gate[:, r].rearrange("p g b d -> p g b d"),
                                                exp_ps[:, r, :].rearrange("p (g b d) -> p g b d", g=2, b=NB),
                                                rows[:, 2 * r * D:2 * (r + 1) * D].rearrange("p (g d) -> p g d", g=2).unsqueeze(2).to_broadcast([P, 2, NB, D]),
                                                ALU.add)
                    ins.then_inc(gates_ready, 1)
                elif name == "ST":
                    dve.wait_ge(x_in[k], 16)
                    statistics(b, k)
                elif name == "XH":
                    i = NORM_NO[(k, c)]
                    dve.wait_ge(rstd_ready, i + 1)
                    for t in range(T):
                        ins = dve.tensor_scalar(xhat[:, i % 2, t, :], x[:, b, t, :], mv[:, i % 2, t, 0:1], rstd[:, i % 2, t:t + 1],
                                                ALU.subtract, ALU.mult)
                    ins.then_inc(xhat_ready, 1)
                elif name == "MK":
                    i = NORM_NO[(k, 1)]
                    dve.wait_ge(late_in, LATE)
                    dve.wait_ge(h_ready, i + 1)
                    if b == 0:
                        settle(dve.tensor_copy(mask_col[:, :, :], mask_u8))
                    dve.tensor_tensor(hT[:, i % 2, :], hT[:, i % 2, :], mask_row[:, b, :], ALU.mult).then_inc(h_masked, 1)
                elif name == "V":
                    if k < NB:
                        dve.wait_ge(v_set[k], 2)
                    dve.wait_ge(dense_full, n + 1)
                    dve.tensor_copy(v_ones[:, b, :, :, 0:HD], bank(n).rearrange("p (t h d) -> p t h d", t=T, d=HD)).then_inc(v_ready, 1)
                elif name in ("RK", "RQ"):
                    m = 0 if name == "RK" else 1
                    r = 2 * (k - NB) + m
                    sin = rot1[:, b, 0, :] if layer == 1 else rot2[:, 0, :]
                    dve.wait_ge(dense_full, n + 1)
                    if k == NB:
                        dve.wait_ge(sincos, 1)
                    settle(dve.tensor_tensor(work[:, 4 + m, :], bank(n), sin, ALU.mult))
                    dve.wait_ge(cos_done, r + 1)
                    dve.tensor_tensor(work[:, m, :], work[:, 2 + m, :], work[:, 4 + m, :], ALU.add).then_inc(roped, 1)
                elif name == "SQ":
                    if layer == 0:
                        dve.wait_ge(qk_ready, 2 * k + 2)
                    else:
                        dve.wait_ge(roped, 2 * (k - NB) + 2)
                    if k > 0:
                        dve.wait_ge(stacked[(k - 1) % 2], 192 * ((k - 1) // 2 + 1))
                    split(work[:, 1, :], work[:, 5, :], 1, split_q)
                elif name == "ANG":
                    dve.wait_ge(dense_full, n + 1)
                    dve.tensor_copy(ang[:, :], bank(n)).then_inc(ang_read, 1)
                    dve.wait_ge(ang_read, k + 1)
                elif name == "RED":
                    bb, f = k // 2, k % 2
                    out = rot1[:, bb, f, :]
                    magic = 12582912.0
                    two_pi_hi = 6.28125
                    two_pi_lo = float(2 * np.pi - 6.28125)
                    pi = 3.1415925
                    settle(dve.tensor_scalar(turns[:, :], ang[:, :], float(1 / (2 * np.pi)), 0.25 * f, ALU.mult, ALU.add))
                    settle(dve.tensor_scalar(turns[:, :], turns[:, :], magic, magic, ALU.add, ALU.subtract))
                    settle(dve.scalar_tensor_tensor(out=out, in0=turns[:, :], scalar=-two_pi_hi, in1=ang[:, :], op0=ALU.mult, op1=ALU.add))
                    settle(dve.scalar_tensor_tensor(out=out, in0=turns[:, :], scalar=-two_pi_lo, in1=out, op0=ALU.mult, op1=ALU.add))
                    settle(dve.tensor_scalar(out, out, float(np.pi / 2) * f, pi, ALU.add, ALU.min))
                    ins = dve.tensor_scalar(out, out, -pi, None, ALU.max)
                    ins.then_inc(ang_ready, 1)
                    dve.wait_ge(ang_ready, k + 1)
                elif name == "OG":
                    g = k % GROUPS
                    src = bank(n).rearrange("p (t j e) -> p t j e", t=T, j=4)
                    dve.wait_ge(dense_full, n + 1)
                    if k > 0:
                        dve.wait_ge(o_ready, k)
                    settle(dve.reciprocal(rden[:, :, :], src[:, :, :, HD]))
                    dve.tensor_tensor(o_tok[:, :, 32 * g:32 * g + 32].rearrange("p t (j d) -> p t j d", d=HD), src[:, :, :, 0:HD],
                                      rden[:, :, :].unsqueeze(3).to_broadcast([P, T, 4, HD]), ALU.mult).then_inc(o_ready, 1)
                elif name in ("WO", "W2", "W2S", "W2F"):
                    src = bank(n).rearrange("p (t d) -> p t d", t=T)
                    dve.wait_ge(dense_full, n + 1)
                    if (name, k) in GATED_NO:
                        r, gi = GATE_OF[(name, layer)]
                        g_tile = gate[:, r, gi, b, :].unsqueeze(1).to_broadcast([P, T, D])
                        dve.tensor_tensor(gated[:, :, :], src, g_tile, ALU.mult).then_inc(res_read, 1)
                        dve.wait_ge(res_read, residual_no[(name, k)])
                        dve.wait_ge(xg_ready, GATED_NO[(name, k)] + 1)
                        if name == "W2S":
                            for t in range(T):
                                ins = dve.scalar_tensor_tensor(out=x[:, b, t, :], in0=gated[:, t, :], scalar=mask_col[:, b, t:t + 1],
                                                               in1=xg[:, b, t, :], op0=ALU.mult, op1=ALU.add)
                        else:
                            ins = dve.tensor_tensor(x[:, b], gated[:, :, :], xg[:, b], ALU.add)
                        if name == "W2F":
                            ins.then_inc(y_ready, 1)
                        else:
                            settle(ins)
                    else:
                        dve.tensor_tensor(x[:, b], src, x[:, b], ALU.add).then_inc(res_read, 1)
                        dve.wait_ge(res_read, residual_no[(name, k)])
                    if name != "W2F":
                        nxt = {"WO": 0, "W2": 1, "W2S": 2}[name]
                        statistics(b, NORM_NO[(k, nxt)])

            zero32 = q_stack[:, 0].rearrange("p h s -> p (h s)").bitcast(F32)
            dve.memset(half[:, 4:5], 0.0).then_inc(zeros_set, 1)
            dve.memset(half[:, 0:T], -0.5).then_inc(id_ready, 1)
            dve.memset(zero32, 0.0).then_inc(stack_zero[0], 1)
            dve.memset(v_ones[:, 0], 0.0).then_inc(v_set[0], 1)
            dve.wait_ge(v_set[0], 1)
            dve.memset(v_ones[:, 0, :, :, HD:HD + 1], 1.0).then_inc(v_set[0], 1)

            for s, i, items in walk():
                if i == 0 and max_rows_of(s) is not None:
                    G = max_rows_of(s)
                    m, r, pt = mx[:, G % 2], mres[:, G % 2], mparts[:, G % 2]
                    dve.wait_ge(tile_free, TILE_USE[("max", s - 1, 3)] + 1)
                    settle(dve.tensor_scalar(pt[:, :, 0, :], m, -1.0, None, ALU.mult))
                    settle(dve.tensor_tensor(r, m, pt[:, :, 0, :], ALU.add))
                    settle(dve.tensor_scalar(pt[:, :, 1, :], r, -1.0, None, ALU.mult))
                    settle(dve.tensor_tensor(r, r, pt[:, :, 1, :], ALU.add))
                    dve.tensor_scalar(pt[:, :, 2, :], r, -1.0, None, ALU.mult).then_inc(max_split, 1)
                if maxima_of(s):
                    q, h = maxima_of(s)
                    G, n = GROUPS * q + h // 4, TILE_USE[("max", s, i)]
                    dve.wait_ge(tile_full, n + 1)
                    dve.tensor_reduce(mx[:, G % 2, i, h % 4:h % 4 + 1], max_ps[:, n % 2, :], AX_X, ALU.max).then_inc(tile_free, 1)
                if i == 2 and max_rows_of(s) is not None:
                    G = max_rows_of(s)
                    n = TILE_USE[("rows", s)]
                    dve.wait_ge(tile_full, n + 1)
                    if G >= 2:
                        dve.wait_ge(rows_in_stack[G % 2], 48 * (G // 2))
                    dve.tensor_copy(mrows[:, G % 2, :], max_ps[0:12, n % 2, :].bitcast(BF16)[:, 0:S]).then_inc(tile_free, 1)
                for item in items:
                    dense(item)

        @block.gpsimd
        def _(pool):
            steps = [0]

            def settle(ins):
                steps[0] += 1
                ins.then_inc(pool_step, 1)
                pool.wait_ge(pool_step, steps[0])

            def inv_std(i, eps):
                pool.wait_ge(stats_ready, i + 1)
                settle(pool.tensor_scalar(rstd[:, i % 2, :], mv[:, i % 2, :, 1], eps, None, ALU.add))
                pool.tensor_tensor(rstd[:, i % 2, :], rstd[:, i % 2, :], half[:, 0:T], ALU.pow).then_inc(rstd_ready, 1)

            def add_bias(step, k):
                layer, b = chain_of_job_layers(k)
                r, gi = GATE_OF[(step, layer)]
                gb = gate_b[:, r, gi, b, :]
                if step == "W2S":
                    for t in range(T):
                        pool.wait_ge(h_masked, b + 1)
                        ins = pool.tensor_scalar(xg[:, b, t, :], gb, mask_col[:, b, t:t + 1], 1.0, ALU.mult, ALU.mult)
                    settle(ins)
                    pool.tensor_tensor(xg[:, b], xg[:, b], x[:, b], ALU.add).then_inc(xg_ready, 1)
                else:
                    pool.tensor_tensor(xg[:, b], x[:, b], gb.unsqueeze(1).to_broadcast([P, T, D]), ALU.add).then_inc(xg_ready, 1)

            def split(src, res, which, done_sem):
                settle(pool.tensor_scalar(parts[:, which, 0, :], src, 1.0, 1.0, ALU.mult, ALU.mult))
                settle(pool.tensor_tensor(res, src, parts[:, which, 0, :], ALU.subtract))
                settle(pool.tensor_scalar(parts[:, which, 1, :], res, 1.0, 1.0, ALU.mult, ALU.mult))
                pool.tensor_tensor(parts[:, which, 2, :], res, parts[:, which, 1, :], ALU.subtract).then_inc(done_sem, 1)

            def dense(item):
                name, k, c = item
                layer, b = chain_of_job_layers(k)
                if name == "ST":
                    if k == 0:
                        pool.wait_ge(id_ready, 1)
                    inv_std(k, EPS[0])
                elif name == "GATE":
                    pool.wait_ge(gates_ready, 1)
                    settle(pool.tensor_tensor(rows[:, 10 * D:11 * D], rows[:, 10 * D:11 * D], rows[:, 11 * D:12 * D], ALU.add))
                    for r in range(3):
                        for gi in range(2):
                            col = (6 + 2 * r + gi) if (r, gi) != (2, 1) else 12
                            ins = pool.tensor_tensor(gate_b[:, r, gi], gate[:, r, gi],
                                                     rows[:, col * D:(col + 1) * D].unsqueeze(1).to_broadcast([P, NB, D]), ALU.mult)
                    ins.then_inc(gate_b_ready, 1)
                elif name == "XG0":
                    pool.wait_ge(gate_b_ready, 1)
                    for bb in range(NB):
                        pool.wait_ge(x_in[bb], 16)
                    add_bias("WO", 2)
                    add_bias("WO", 3)
                    pool.wait_ge(late_in, LATE)
                    pool.tensor_copy(pos_f[:, :, :], pos_i[:, :, :]).then_inc(pos_ready, 1)
                elif name in ("K", "Q") and layer > 0:
                    m = 0 if name == "K" else 1
                    cos = rot1[:, b, 1, :] if layer == 1 else rot2[:, 1, :]
                    if k == NB and m == 0:
                        pool.wait_ge(sincos, 1)
                        pool.wait_ge(late_in, LATE)
                    pool.wait_ge(qk_ready, 2 * k + 1 + m)
                    pool.tensor_tensor(work[:, 2 + m, :], work[:, m, :], cos, ALU.mult).then_inc(cos_done, 1)
                elif name == "RK" or (name == "K" and layer == 0):
                    if layer == 0:
                        pool.wait_ge(qk_ready, 2 * k + 1)
                    else:
                        pool.wait_ge(roped, 2 * (k - NB) + 1)
                    if k > 0:
                        pool.wait_ge(stacked[(k - 1) % 2], 192 * ((k - 1) // 2 + 1))
                    split(work[:, 0, :], work[:, 4, :], 0, split_k)
                elif name in ("WO", "W2", "W2S"):
                    i = NORM_NO[(k, {"WO": 0, "W2": 1, "W2S": 2}[name])]
                    inv_std(i, EPS[layer - 1] if name == "WO" else EPS[layer])
                    nxt = next_gated(name, k)
                    if nxt:
                        add_bias(*nxt)

            flat = [k_stack[:, b].rearrange("p h s -> p (h s)").bitcast(F32) for b in range(NB)]
            one_pair = float(np.array([0x3F803F80], np.uint32).view(np.float32)[0])
            pool.memset(flat[0], 0.0).then_inc(stack_zero[0], 1)
            for s, i, items in walk():
                for item in items:
                    dense(item)
                    if item[0] == "ST" and item[1] == 1:
                        pool.wait_ge(v_set[1], 1)
                        pool.memset(v_ones[:, 1, :, :, HD:HD + 1], 1.0).then_inc(v_set[1], 1)
                        pool.wait_ge(v_set[1], 2)
                        for b in range(NB):
                            pool.wait_ge(stack_zero[b], 2)
                            pool.memset(flat[b][MAX_ROW:MAX_ROW + 3], one_pair).then_inc(ones_set, 1)
                            pool.wait_ge(ones_set, b + 1)


def lay_out(a):
    f = np.float32

    def vecs(*cols):
        return [np.asarray(c, f).reshape(-1, P) for c in cols]

    def heads_inner(m):
        return m.reshape(m.shape[:-1] + (H, HD)).swapaxes(-1, -2).reshape(m.shape)

    def layer(wq, wk, wv, wo, w1, w2):
        return np.concatenate([heads_inner(wq), heads_inner(wk), wv, wo, w1, rows_by_tile(w2)], 1)

    def rows_by_tile(m):
        return m.reshape(-1, P, m.shape[1]).transpose(1, 0, 2).reshape(P, -1)

    b0, b1, b3, b3f = a["L0_cond_b_ada"], a["L1_cond_ada_b"], a["L3_cond_ada_b"], a["L3_cond_ffada_b"]
    zero, one = np.zeros(P, f), np.ones(P, f)
    qkv_w, qkv_b = a["L1_cond_qkv_w"], a["L1_cond_qkv_b"]
    shift_scale = [b[c * D:(c + 1) * D] for b, cs in ((b0, (0, 1, 3, 4)), (b1, (0, 1, 3, 4))) for c in cs]
    shift_scale += [zero, zero] + [b[c * D:(c + 1) * D] for b in (b3, b3f) for c in (0, 1)]
    ones = [one if m % 2 == 1 and m != 9 else zero for m in range(MOD)]
    vec = vecs(*shift_scale, *ones,
               heads_inner(a["L0_cond_bq"]), heads_inner(a["L0_cond_bk"]), a["L0_cond_bv"],
               heads_inner(qkv_b[0:D]), heads_inner(qkv_b[D:2 * D]), qkv_b[2 * D:],
               a["L0_cond_b1"], a["L1_cond_fc1_b"], a["L2_cond_mlp_ln_scale"], a["L3_cond_ssm_b1"], a["L3_cond_bwd_b1"],
               a["L3_cond_ff_b1"])
    vec = np.concatenate(vec, 0)
    pad = np.zeros((V_N - len(vec), P), f)
    vec = np.concatenate([vec, pad], 0).T
    ada = np.concatenate([a["L0_cond_W_ada"], a["L1_cond_ada_w"], a["L2_cond_w_offset"], a["L2_cond_w_scale"],
                          a["L3_cond_ada_w"], a["L3_cond_ffada_w"]], 1)
    gates = [b0[2 * D:3 * D], b0[5 * D:], b1[2 * D:3 * D], b1[5 * D:], b3[2 * D:], b3f[2 * D:]]
    rows = np.concatenate(gates + [a["L0_cond_bo"], a["L0_cond_b2"], a["L1_cond_proj_b"], a["L1_cond_fc2_b"],
                                   a["L3_cond_ssm_b2"], a["L3_cond_bwd_b2"], a["L3_cond_ff_b2"]])[None, :]
    turn = np.zeros((P, 2, P), f)
    freq = np.zeros((2, P), f)
    inv1 = (f(1.0) / f(100.0) ** (np.arange(0, 4, 2, dtype=f) / f(4))).astype(f)
    inv2 = (f(10000.0) ** (-np.arange(0, HD, 2, dtype=f) / f(HD))).astype(f)
    grid = np.arange(S, dtype=f)[:, None] * inv2[None, :]
    rot2 = np.zeros((P, 2, S), f)
    for d in range(HD):
        for h in range(H):
            to = d * H + h
            turn[(d + 2 if d % 4 < 2 else d - 2) * H + h, 0, to] = -1 if d % 4 < 2 else 1
            turn[(d + 1 if d % 2 == 0 else d - 1) * H + h, 1, to] = -1 if d % 2 == 0 else 1
            freq[d // 4, to] = inv1[d % 2]
            rot2[to, 0], rot2[to, 1] = np.sin(grid[:, d // 2].astype(np.float64)), np.cos(grid[:, d // 2].astype(np.float64))
    mask = a["mask_BxS_bk0"].view(np.uint8)
    return {
        "x": a["x"], "cond": a["cond_1024"].T, "vec": vec, "ident": np.eye(P, dtype=f), "ada": ada, "rows": rows,
        "turn": turn, "freq": freq, "rot2": rot2,
        "pos": a["itok_BxSx2_0_63"].transpose(2, 0, 1), "mask_row": mask.view(np.int32),
        "mask_col": np.ascontiguousarray(mask.reshape(NB, T, P).transpose(2, 0, 1)).reshape(P, NB * T).view(np.int32),
        "w0": layer(*[a["L0_cond_" + n] for n in ("Wq", "Wk", "Wv", "Wo", "W1", "W2")]),
        "w1": layer(qkv_w[:, 0:D], qkv_w[:, D:2 * D], qkv_w[:, 2 * D:], a["L1_cond_proj_w"], a["L1_cond_fc1_w"], a["L1_cond_fc2_w"]),
        "w2": layer(*[a["L2_cond_" + n] for n in ("wq", "wk", "wv", "wo", "w1", "w2")]),
        "w3": np.concatenate([a["L3_cond_ssm_w1"], a["L3_cond_bwd_w1"], a["L3_cond_ssm_w2"], a["L3_cond_bwd_w2"],
                              a["L3_cond_ff_w1"], rows_by_tile(a["L3_cond_ff_w2"])], 1),
    }


def kernel(**inputs):
    import concourse.bacc as bacc
    from concourse.bass_utils import run_bass_kernel_spmd

    nc = bacc.Bacc("TRN2", target_bir_lowering=False, num_devices=1)
    arrays, ins = {}, {}
    for name, a in lay_out({n: np.asarray(v) for n, v in inputs.items()}).items():
        a = np.ascontiguousarray(a)
        arrays[f"in_{name}_dram"] = a
        ins[name] = nc.dram_tensor(f"in_{name}_dram", a.shape, mybir.dt.from_np(a.dtype), kind="ExternalInput").ap()
    y = nc.dram_tensor("out_0_dram", (NB, S, D), F32, kind="ExternalOutput").ap()
    build(nc, ins, y)
    r = run_bass_kernel_spmd(nc, [arrays], core_ids=[0])
    return r.results[0]["out_0_dram"]
```

```python
from contextlib import ExitStack

import numpy as np

import concourse.bass as bass
from concourse import mybir

F32 = mybir.dt.float32
BF16 = mybir.dt.bfloat16
I32 = mybir.dt.int32
U8 = mybir.dt.uint8
ALU = mybir.AluOpType
ACT = mybir.ActivationFunctionType
AX_X = mybir.AxisListType.X

P = 128
NB, S, D, H, HD, FF = 2, 512, 128, 16, 8, 512
T = S // P
LAYERS = 3
CHAINS = LAYERS * NB
GROUPS = H // 4
SCORE_SCALE = [HD ** -0.5, HD ** -0.5, D ** -0.5]
EPS = [1e-5, 1e-6, 1e-5, 1e-6]
PARTS_Q = [0, 0, 0, 1, 1, 2]
PARTS_K = [0, 1, 2, 0, 1, 0]
STACK_K, STACK_Q = 16 * len(PARTS_K), 16 * (len(PARTS_Q) + 1)
ZERO_ROW = 8 * len(PARTS_K)
MAX_ROW = 96
TILES = 4
RING_P = 12

MOD = 14
V_BIAS, V_ONE, V_BQ, V_BK, V_BV, V_B1, V_LN2, V_SSM1, V_FF1, V_ZERO, V_N = 0, 14, [28, 31, 50], [29, 32, 50], [30, 33, 50], [34, 38, None], 42, 43, 45, 50, 51
W_Q, W_K, W_V, W_O, W_1, W_2 = 0, 128, 256, 384, 512, 1024
STRIDE = 17
LAG_B = 6
LAG_V = 1
OG_LAG = 2
JOB_LAG = 6
JOB1_AT = 0
ANG_AT = 30


def chain_of_job_layers(k):
    return k // NB, k % NB


GAP = {"OT": 2, "WO": 1, "SX": 2, "XH": 2, "TR": 2, "W1": 1, "W2": 0, "MK": 4, "ST": 8, "K": 1, "Q": 1, "V": 0, "RK": 2, "RQ": 1, "SQ": 0, "DK": 1, "DQ": 1}
CHUNKS = {"W1": 4, "W1S": 2, "W1F": 2}


def gap(name):
    return GAP[name[:2]]


def mlp(kind):
    return ["W1" + kind] + ["W2" + kind] * T


def dense_items(k):
    layer = k // NB
    items = []
    if layer > 0:
        items += ["OT", "WO", "SX", "XH", "TR"] + mlp("") + ["SX", "XH", "TR"]
    if layer == LAYERS:
        return items + ["MK"] + mlp("S") + ["SX", "XH", "TR"] + mlp("F")
    if layer == 0:
        items += ["ST", "XH", "TR"]
    items += ["K", "Q"]
    if layer > 0:
        items += ["RK", "RQ"]
    return items + ["SQ"] + ["DK"] * 3 + ["DQ"] * 3 + ["V"]


PLACES = (0, 2, 3)


def make_plan():
    last = STRIDE * (CHAINS - 1) + LAG_B + H + LAG_V + 1
    plan = [[[] for _ in PLACES] for _ in range(last + 60)]

    def put(at, item):
        plan[at // 3][at % 3].append(item)
        return at

    def put_job(k, at, items=None):
        for name in items or dense_items(k):
            put(at, (name, k))
            at += gap(name)
        return at

    plan[0][0] = [(name, 0) for name in dense_items(0)] + [("ADA1", 0), ("GATE", 0)]
    plan[0][0].insert(1, ("ADA0", 0))
    end = put_job(1, JOB1_AT)
    put(3 * 5, ("XG0", 0))
    at = ANG_AT
    for b in range(NB):
        put(at, ("ANG", b)); at += 1
        for f in range(2):
            put(at, ("RED", 2 * b + f)); at += 3
    put(at + 3, ("SIN", 0))
    for q in range(CHAINS):
        for g in range(GROUPS):
            put(3 * (first_slot(q) + LAG_B + 4 * g + 3 + LAG_V) + OG_LAG, ("OG", GROUPS * q + g))
        k = q + NB
        start = 3 * (first_slot(q) + LAG_B + H - 1 + LAG_V) + JOB_LAG
        end = put_job(k, max(start, end))
    used = max(s for s, sl in enumerate(plan) if any(sl))
    return plan[:used + 1]


def first_slot(q):
    return 1 + STRIDE * q


PLAN = make_plan()
SLOTS = len(PLAN)


def maxima_of(s):
    for q in range(CHAINS):
        if 0 <= s - first_slot(q) < H:
            return q, s - first_slot(q)
    return None


def exps_of(s):
    for q in range(CHAINS):
        n = s - first_slot(q) - LAG_B
        if 0 <= n < H:
            return GROUPS * q + n // 4, n % 4
    return None


def max_rows_of(s):
    for q in range(CHAINS):
        n = s - first_slot(q)
        if n in (4, 8, 12, 16):
            return GROUPS * q + n // 4 - 1
    return None


def banks_of(name):
    if name in CHUNKS:
        return CHUNKS[name]
    return int(name in ("ADA0", "ADA1", "OG", "OT", "WO", "TR", "W2", "W2S", "W2F", "K", "Q", "V", "RK", "RQ", "ANG"))


def number_uses():
    use, seen, maxima, n = {}, {}, [], 0
    for s in range(SLOTS):
        for i in range(4):
            if maxima_of(s):
                use[("max", s, i)] = n
                maxima.append(n)
                n += 1
            if i == 2 and max_rows_of(s) is not None:
                use[("rows", s)] = n
                maxima.append(n)
                n += 1
            if i in PLACES:
                for item in PLAN[s][PLACES.index(i)]:
                    c = seen.get(item, 0)
                    seen[item] = c + 1
                    use[item + (c,)] = n
                    n += banks_of(item[0])
    return use, maxima


USE, MAXIMA_USES = number_uses()


def walk():
    seen = {}
    for s in range(SLOTS):
        for i in range(4):
            items = []
            if i in PLACES:
                for item in PLAN[s][PLACES.index(i)]:
                    n = seen.get(item, 0)
                    seen[item] = n + 1
                    items.append((item[0], item[1], n))
            yield s, i, items


def next_gated(k, c):
    layer = k // NB
    return {(1, 0): ("W2", k), (1, 1): ("WO", k + NB), (2, 0): ("W2", k), (3, 1): ("W2S", k), (3, 2): ("W2F", k)}.get((layer, c))


def norm_order():
    norm_no, n = {}, 0
    gated_no, g = {}, 0
    for _, _, items in walk():
        for name, k, c in items:
            if name in ("ST", "SX"):
                norm_no[(k, c)] = n
                n += 1
            if name == "XG0":
                gated_no[("WO", 2)], gated_no[("WO", 3)] = g, g + 1
                g += 2
            layer = k // NB
            nxt = next_gated(k, c) if name == "SX" else None
            if nxt:
                gated_no[nxt] = g
                g += 1
    return norm_no, gated_no


NORM_NO, GATED_NO = norm_order()
GATE_OF = {("WO", 1): (0, 0), ("W2", 1): (0, 1), ("WO", 2): (1, 0), ("W2", 2): (1, 1), ("W2S", 3): (2, 0), ("W2F", 3): (2, 1)}


def build(nc, ins, y):
    ctx = ExitStack()
    with ctx:
        def sb(name, shape, dt=F32):
            return ctx.enter_context(nc.sbuf_tensor(name, shape, dt))

        def sem(name):
            return ctx.enter_context(nc.semaphore(name))

        x = sb("x", [P, NB, T, D])
        xg = sb("xg", [P, NB, T, D])
        q_stack = sb("q_stack", [P, NB, H, S], BF16)
        k_stack = sb("k_stack", [P, NB, H, S], BF16)
        v_ones = sb("v_ones", [P, NB, T, H, 32])
        probs = sb("probs", [P, RING_P, S])
        w = [sb(f"w{n}", [P, 1536 if n < LAYERS else 1024]) for n in range(LAYERS + 1)]
        vec = sb("vec", [P, V_N])
        modv = sb("modv", [P, MOD, NB])
        gate = sb("gate", [P, 3, 2, NB, D])
        gate_b = sb("gate_b", [P, 3, 2, NB, D])
        ident = sb("ident", [P, P])
        ident_bf = sb("ident_bf", [P, P], BF16)
        turn = sb("turn", [P, 2, P])
        freq = sb("freq", [2, P])
        pos_i = sb("pos_i", [2, NB, S], I32)
        pos_f = sb("pos_f", [2, NB, S])
        rot1 = sb("rot1", [P, NB, 2, S])
        rot2 = sb("rot2", [P, 2, S])
        mask_words = sb("mask_words", [P, NB, S // 4], I32)
        mask_row = mask_words[:, :, :].bitcast(U8)
        mask_col_words = sb("mask_col_words", [P, NB * T // 4], I32)
        mask_u8 = mask_col_words[:, :].bitcast(U8).rearrange("p (b t) -> p b t", b=NB)
        mask_col = sb("mask_col", [P, NB, T])
        cond = sb("cond", [P, NB])
        silu = sb("silu", [P, 4, NB])
        xhat = sb("xhat", [P, 2, T, D])
        hT = sb("hT", [P, 2, S])
        work = sb("work", [P, 6, S])
        hid = work[:, 0:4]
        parts = sb("parts", [P, 2, 3, S], BF16)
        oT_raw = sb("oT_raw", [P, S])
        o_tok = sb("o_tok", [P, T, D])
        oT = sb("oT", [P, S])
        rden = sb("rden", [P, T, 4])
        gated = work[:, 5].rearrange("p (t d) -> p t d", t=T)
        bst = sb("bst", [P, T, 6])
        mv = sb("mv", [P, 2, T, 2])
        rstd = sb("rstd", [P, 2, T])
        half = sb("half", [P, 5])
        mx = sb("mx", [P, 2, T, 4])
        mres = sb("mres", [P, 2, T, 4])
        mparts = sb("mparts", [P, 2, T, 3, 4], BF16)
        ones_rows = sb("ones_rows", [3, S], BF16)
        mrows = sb("mrows", [12, 2, S], BF16)
        ang, turns = work[:, 2], work[:, 3]
        pflat = probs[:, :, :].rearrange("p a b -> p (a b)")
        ada = pflat[:, 0:2560]
        rows = pflat[:, 2560:2560 + 13 * D]
        cwide = pflat[:, 4608:4608 + 4 * P].rearrange("p (a n) -> p a n", a=4)

        ring_ps = ctx.enter_context(nc.psum_tensor("ring_ps", [P, TILES, S], F32))
        exp_ps = ctx.enter_context(nc.psum_tensor("exp_ps", [P, 3, S], F32))
        pv_ps = ctx.enter_context(nc.psum_tensor("pv_ps", [P, S], F32))

        x_in = [sem(f"x{b}_in") for b in range(NB)]
        small_in, ada0_in, ada1_in, rows_in = sem("small_in"), sem("ada0_in"), sem("ada1_in"), sem("rows_in")
        w_in = [sem(f"w{n}_in") for n in range(LAYERS + 1)]
        late_in = sem("late_in")
        stack_zero = [sem(f"stack_zero{b}") for b in range(NB)]
        v_set = [sem(f"v_set{b}") for b in range(NB)]
        zeros_set, ones_tile_set = sem("zeros_set"), sem("ones_tile_set")
        ones_set = [sem(f"ones_set{b}") for b in range(NB)]
        stacked_k = [sem(f"stacked_k{b}") for b in range(NB)]
        stacked_q = [sem(f"stacked_q{b}") for b in range(NB)]
        tile_full, tile_free = sem("tile_full"), sem("tile_free")
        max_split = sem("max_split")
        rows_in_stack = [sem(f"rows_in_stack{n}") for n in range(2)]
        shifted, exp_done, quad_done, quad_out = sem("shifted"), sem("exp_done"), sem("quad_done"), sem("quad_out")
        v_ready, o_ready = sem("v_ready"), sem("o_ready")
        gelu_done = sem("gelu_done")
        x_ready = sem("x_ready")
        res_read, ang_read = sem("res_read"), sem("ang_read")
        cond_ready, silu_exp, mod_ready = sem("cond_ready"), sem("silu_exp"), sem("mod_ready")
        gates_full, gates_ready, gate_b_ready = sem("gates_full"), sem("gates_ready"), sem("gate_b_ready")
        id_ready, pos_ready, ang_ready, sincos = sem("id_ready"), sem("pos_ready"), sem("ang_ready"), sem("sincos")
        stats_ready, rstd_ready, xhat_ready, h_ready, h_masked = sem("stats_ready"), sem("rstd_ready"), sem("xhat_ready"), sem("h_ready"), sem("h_masked")
        qk_ready, cos_done, roped, split_k, split_q = sem("qk_ready"), sem("cos_done"), sem("roped"), sem("split_k"), sem("split_q")
        oT_ready, hid_ready, xg_ready, y_ready, y_out = sem("oT_ready"), sem("hid_ready"), sem("xg_ready"), sem("y_ready"), sem("y_out")
        dve_step, pool_step = sem("dve_step"), sem("pool_step")

        def bank(n):
            return ring_ps[:, n % TILES, :]

        def mlp_weights(name, layer):
            if name in ("W1", "W2"):
                t = w[layer - 1]
                return t[:, W_1:W_1 + FF], t[:, W_2:W_2 + FF]
            t = w[LAYERS]
            return (t[:, 0:256], t[:, 256:512]) if name in ("W1S", "W2S") else (t[:, 512:768], t[:, 768:1024])

        def norm_of(name, k):
            layer = k // NB
            if layer == 0:
                return NORM_NO[(k, 0)]
            if name == "W1":
                return NORM_NO[(k, 0)]
            if name == "W1F":
                return NORM_NO[(k, 2)]
            return NORM_NO[(k, 1)]

        read_of = {n: (tile_free, m + 1) for m, n in enumerate(MAXIMA_USES)}
        gelu_no, residual_no, x_written = {}, {}, {}
        gelus = residuals = written = 0
        for _, _, items in walk():
            for name, k, c in items:
                n = USE[(name, k, c)]
                if name in CHUNKS:
                    for j in range(CHUNKS[name]):
                        gelus += 1
                        read_of[n + j] = (gelu_done, gelus)
                    gelu_no[(name, k)] = gelus
                elif name == "WO" or name[:2] == "W2":
                    residuals += 1
                    residual_no[(name, k, c)] = residuals
                    read_of[n] = (res_read, residuals)
                    if name == "WO" or (c == T - 1 and name != "W2F"):
                        gated_step = (name, k) in GATED_NO
                        written += gated_step
                        x_written[k, {"WO": 0, "W2": 1, "W2S": 2}[name]] = (x_ready, written) if gated_step else (res_read, residuals)
                elif banks_of(name):
                    read_of[n] = {
                        "ADA0": (mod_ready, 1), "ADA1": (mod_ready, 2), "V": (v_ready, k + 1), "OG": (o_ready, k + 1),
                        "TR": (h_ready, NORM_NO.get((k, c), 0) + 1), "K": (qk_ready, 2 * k + 1), "Q": (qk_ready, 2 * k + 2),
                        "OT": (oT_ready, k - NB + 1), "ANG": (ang_read, k + 1),
                        "RK": (roped, 2 * (k - NB) + 1), "RQ": (roped, 2 * (k - NB) + 2),
                    }[name]

        block = ctx.enter_context(nc.Block())

        @block.sync
        def _(sp):
            sp.dma_start(x[:, 0], ins["x"][0].rearrange("(t p) d -> p t d", p=P)).then_inc(x_in[0], 16)
            sp.dma_start(cond[:, :], ins["cond"]).then_inc(small_in, 16)
            sp.dma_start(vec[:, :], ins["vec"]).then_inc(small_in, 16)
            sp.dma_start(ident[:, :], ins["ident"]).then_inc(small_in, 16)
            sp.dma_start(ada[:, 0:768], ins["ada"][:, 0:768]).then_inc(ada0_in, 16)
            sp.dma_start(w[0][:, 0:512], ins["w0"][:, 0:512]).then_inc(w_in[0], 16)
            sp.dma_start(x[:, 1], ins["x"][1].rearrange("(t p) d -> p t d", p=P)).then_inc(x_in[1], 16)
            sp.dma_start(ada[:, 768:2560], ins["ada"][:, 768:2560]).then_inc(ada1_in, 16)
            sp.dma_start(rows, ins["rows"].to_broadcast([P, 13 * D])).then_inc(rows_in, 16)

            def stack(k, which, part, target, of_part, split_done, done):
                layer, b = chain_of_job_layers(k)
                sp.wait_ge(split_done, 3 * k + part + 1)
                for r in range(len(of_part)):
                    if of_part[r] == part:
                        sp.dma_start(target[8 * r:8 * r + 8, b], parts[:, which, part, :]).then_inc(done[b], 16)

            for s, i, items in walk():
                if i == 3 and max_rows_of(s) is not None:
                    G = max_rows_of(s)
                    b = (G // GROUPS) % NB
                    sp.wait_ge(*read_of[USE[("rows", s)]])
                    sp.dma_start(q_stack[MAX_ROW:MAX_ROW + 3, b, 4 * (G % GROUPS):4 * (G % GROUPS) + 4, :],
                                 mrows[:, G % 2, :]).then_inc(rows_in_stack[G % 2], 16)
                for name, k, c in items:
                    if name == "DK":
                        if k < NB and c == 0:
                            sp.wait_ge(stack_zero[k], 2)
                            sp.wait_ge(ones_tile_set, 1)
                            sp.dma_start(k_stack[MAX_ROW:MAX_ROW + 3, k], ones_rows[:, :].unsqueeze(1).to_broadcast([3, H, S])).then_inc(ones_set[k], 16)
                        stack(k, 0, c, k_stack, PARTS_K, split_k, stacked_k)
                    if name == "DQ":
                        b = k % NB
                        if c == 0:
                            sp.dma_start(q_stack[MAX_ROW:MAX_ROW + 3, b], k_stack[ZERO_ROW:ZERO_ROW + 3, b]).then_inc(stacked_q[b], 16)
                        stack(k, 1, c, q_stack, PARTS_Q, split_q, stacked_q)
                        if k == 0 and c == 2:
                            sp.dma_start(w[0][:, 512:1536], ins["w0"][:, 512:1536]).then_inc(w_in[0], 16)
                            sp.dma_start(turn[:, :, :], ins["turn"]).then_inc(late_in, 16)
                            sp.dma_start(freq[:, :], ins["freq"]).then_inc(late_in, 16)
                            sp.dma_start(pos_i[:, :, :], ins["pos"]).then_inc(late_in, 16)
                            sp.dma_start(rot2[:, :, :], ins["rot2"]).then_inc(late_in, 16)
                            for b in range(NB):
                                sp.dma_start(mask_words[:, b, :], ins["mask_row"][b:b + 1, :].to_broadcast([P, S // 4])).then_inc(late_in, 16)
                            sp.dma_start(mask_col_words[:, :], ins["mask_col"]).then_inc(late_in, 16)
                            for n in range(1, LAYERS + 1):
                                sp.dma_start(w[n][:, :], ins[f"w{n}"]).then_inc(w_in[n], 16)
            for b in range(NB):
                sp.wait_ge(y_ready, b + 1)
                sp.dma_start(y[b].rearrange("(t p) d -> p t d", p=P), x[:, b]).then_inc(y_out, 16)
            sp.wait_ge(y_out, 16 * NB)
        LATE = 16 * 7

        @block.tensor
        def _(pe):
            def take(n):
                if n >= TILES:
                    pe.wait_ge(*read_of[n - TILES])

            def turn_tiles(n, src):
                for t in range(T):
                    mm = pe.transpose(bank(n)[:, t * P:(t + 1) * P], src(t), ident[:, :])
                mm.then_inc(tile_full, 1)

            def token_product(n, lhs, weights):
                for t in range(T):
                    mm = pe.matmul(bank(n)[:, t * D:(t + 1) * D], lhs[:, t * P:(t + 1) * P], weights, start=True, stop=True)
                mm.then_inc(tile_full, 1)

            def dense(item):
                name, k, c = item
                layer, b = chain_of_job_layers(k)
                n = USE[item]
                if name == "ADA0":
                    pe.wait_ge(ada0_in, 16)
                    pe.wait_ge(small_in, 48)
                    take(n)
                    for m, col in enumerate((0, 1, 3, 4)):
                        mm = pe.matmul(bank(n)[:, 2 * m:2 * m + 2], ada[:, col * D:(col + 1) * D], cond[:, :], start=True, stop=True)
                    mm.then_inc(tile_full, 1)
                elif name == "ADA1":
                    pe.wait_ge(ada1_in, 16)
                    pe.wait_ge(cond_ready, 2)
                    take(n)
                    cols = [(6, 1), (7, 1), (9, 1), (10, 1), (12, 0), (13, 0), (14, 1), (15, 1), (17, 1), (18, 1)]
                    for m, (col, act) in enumerate(cols):
                        rhs = silu[:, 3, :] if act else cond[:, :]
                        mm = pe.matmul(bank(n)[:, 2 * m:2 * m + 2], ada[:, col * D:(col + 1) * D], rhs, start=True, stop=True)
                    mm.then_inc(tile_full, 1)
                elif name == "GATE":
                    pe.wait_ge(cond_ready, 3)
                    for r, (cols, act) in enumerate((((2, 5), 0), ((8, 11), 1), ((16, 19), 1))):
                        for g, col in enumerate(cols):
                            for bb in range(NB):
                                o = (2 * g + bb) * D
                                mm = pe.matmul(exp_ps[:, r, o:o + D], cwide[:, 2 * act + bb, :], ada[:, col * D:(col + 1) * D], start=True, stop=True)
                    mm.then_inc(gates_full, 1)
                elif name == "TR":
                    i = NORM_NO[(k, c)]
                    pe.wait_ge(xhat_ready, i + 1)
                    take(n)
                    turn_tiles(n, lambda t: xhat[:, i % 2, t, :])
                elif name in ("K", "Q"):
                    i = norm_of(name, k)
                    pe.wait_ge(h_ready, i + 1)
                    pe.wait_ge(w_in[layer], 16)
                    take(n)
                    o = W_K if name == "K" else W_Q
                    pe.matmul(bank(n), w[layer][:, o:o + D], hT[:, i % 2, :], start=True, stop=True).then_inc(tile_full, 1)
                elif name == "V":
                    i = norm_of(name, k)
                    pe.wait_ge(h_ready, i + 1)
                    take(n)
                    token_product(n, hT[:, i % 2, :], w[layer][:, W_V:W_V + D])
                elif name in ("RK", "RQ"):
                    pe.wait_ge(qk_ready, 2 * k + (1 if name == "RK" else 2))
                    if k == NB:
                        pe.wait_ge(late_in, LATE)
                    take(n)
                    pe.matmul(bank(n), turn[:, layer - 1, :], work[:, 0 if name == "RK" else 1, :], start=True, stop=True).then_inc(tile_full, 1)
                elif name == "ANG":
                    pe.wait_ge(pos_ready, 1)
                    take(n)
                    pe.matmul(bank(n), freq[:, :], pos_f[:, k, :], start=True, stop=True).then_inc(tile_full, 1)
                elif name == "OG":
                    pe.wait_ge(quad_out, k + 1)
                    take(n)
                    turn_tiles(n, lambda t: oT_raw[:, t * P:(t + 1) * P])
                elif name == "OT":
                    q = k - NB
                    pe.wait_ge(o_ready, GROUPS * (q + 1))
                    take(n)
                    turn_tiles(n, lambda t: o_tok[:, t, :])
                elif name == "WO":
                    pe.wait_ge(oT_ready, k - NB + 1)
                    take(n)
                    token_product(n, oT, w[layer - 1][:, W_O:W_O + D])
                elif name in CHUNKS:
                    i = norm_of(name, k)
                    if name == "W1S":
                        pe.wait_ge(h_masked, b + 1)
                    else:
                        pe.wait_ge(h_ready, i + 1)
                    if name == "W1":
                        pe.wait_ge(w_in[layer - 1], 32 if layer == 1 else 16)
                    else:
                        pe.wait_ge(w_in[LAYERS], 16)
                    w1, _ = mlp_weights(name, layer)
                    for j in range(CHUNKS[name]):
                        take(n + j)
                        pe.matmul(bank(n + j), w1[:, j * P:(j + 1) * P], hT[:, i % 2, :], start=True, stop=True).then_inc(tile_full, 1)
                elif name[:2] == "W2":
                    chunks = CHUNKS["W1" + name[2:]]
                    _, w2 = mlp_weights(name, layer)
                    if c == 0:
                        pe.wait_ge(gelu_done, gelu_no["W1" + name[2:], k])
                    take(n)
                    for j in range(chunks):
                        mm = pe.matmul(bank(n)[:, 0:D], hid[:, j, c * P:(c + 1) * P], w2[:, j * D:(j + 1) * D],
                                       start=(j == 0), stop=(j == chunks - 1))
                    mm.then_inc(tile_full, 1)

            for s, i, items in walk():
                if exps_of(s):
                    G, kt = exps_of(s)
                    q, g = G // GROUPS, G % GROUPS
                    b, h, n = q % NB, 4 * g + i, 16 * G + 4 * kt + i
                    if kt == 0 and i == 0:
                        pe.wait_ge(rows_in_stack[G % 2], 16 * (G // 2 + 1))
                        if G == 0:
                            pe.wait_ge(gates_ready, 1)
                    if n >= 3:
                        pe.wait_ge(exp_done, n - 2)
                    pe.matmul(exp_ps[:, n % 3, :], k_stack[:, b, h, kt * P:(kt + 1) * P], q_stack[:, b, h, :],
                              start=True, stop=True).then_inc(shifted, 1)
                if maxima_of(s):
                    q, h = maxima_of(s)
                    b, n = q % NB, USE[("max", s, i)]
                    if h == 0 and i == 0:
                        if q < NB:
                            pe.wait_ge(ones_set[b], 16)
                        pe.wait_ge(stacked_k[b], STACK_K * (q // NB + 1))
                        pe.wait_ge(stacked_q[b], STACK_Q * (q // NB + 1))
                    take(n)
                    pe.matmul(ring_ps[:, n % TILES, :], q_stack[:, b, h, i * P:(i + 1) * P], k_stack[:, b, h, :],
                              start=True, stop=True).then_inc(tile_full, 1)
                if i == 1 and exps_of(s - LAG_V):
                    G, kt = exps_of(s - LAG_V)
                    q, g = G // GROUPS, G % GROUPS
                    b = q % NB
                    pe.wait_ge(exp_done, 16 * G + 4 * kt + 4)
                    if kt == 0:
                        pe.wait_ge(v_ready, q + 1)
                        if G > 0:
                            pe.wait_ge(quad_out, G)
                    for j in range(4):
                        n = 16 * G + 4 * kt + j
                        mm = pe.matmul(pv_ps[32 * j:32 * j + 32, :], v_ones[:, b, kt, 4 * g + j, :], probs[:, n % RING_P, :],
                                       start=(kt == 0), stop=(kt == T - 1))
                    mm.then_inc(quad_done, 1)
                if i == 2 and max_rows_of(s) is not None:
                    G = max_rows_of(s)
                    n = USE[("rows", s)]
                    pe.wait_ge(max_split, G + 1)
                    take(n)
                    out = ring_ps[:, n % TILES, :].bitcast(BF16)
                    for t in range(T):
                        mm = pe.transpose(out[0:12, t * P:(t + 1) * P], mparts[:, G % 2, t].rearrange("p a b -> p (a b)"), ident_bf[:, :])
                    mm.then_inc(tile_full, 1)
                for item in items:
                    dense(item)

        @block.scalar
        def _(act):
            def dense(item):
                name, k, c = item
                layer, b = chain_of_job_layers(k)
                n = USE[item]
                if name == "ADA0":
                    act.wait_ge(small_in, 48)
                    act.activation(silu[:, 0, :], cond[:, :], ACT.Exp, scale=-1.0).then_inc(silu_exp, 1)
                elif name == "TR":
                    i = NORM_NO[(k, c)]
                    if layer == 0:
                        act.wait_ge(mod_ready, 1)
                        sh, sc = modv[:, 0, b:b + 1], modv[:, 1, b:b + 1]
                    else:
                        act.wait_ge(mod_ready, 2)
                        cols = {(1, 0): 2, (1, 1): 4, (2, 0): 6, (2, 1): 8, (3, 1): 10, (3, 2): 12}.get((layer, c))
                        if cols is None:
                            sh, sc = vec[:, V_ZERO:V_ZERO + 1], vec[:, V_LN2:V_LN2 + 1]
                        else:
                            sh, sc = modv[:, cols, b:b + 1], modv[:, cols + 1, b:b + 1]
                    act.wait_ge(tile_full, n + 1)
                    act.activation(hT[:, i % 2, :], bank(n), ACT.Identity, bias=sh, scale=sc).then_inc(h_ready, 1)
                elif name in ("K", "Q"):
                    col = (V_BK if name == "K" else V_BQ)[layer]
                    act.wait_ge(tile_full, n + 1)
                    act.activation(work[:, 0 if name == "K" else 1, :], bank(n), ACT.Identity, bias=vec[:, col:col + 1]).then_inc(qk_ready, 1)
                elif name == "OT":
                    col = V_BV[layer - 1]
                    act.wait_ge(tile_full, n + 1)
                    act.activation(oT[:, :], bank(n), ACT.Identity, bias=vec[:, col:col + 1]).then_inc(oT_ready, 1)
                elif name == "V":
                    if k < NB:
                        act.wait_ge(v_set[k], 2)
                    act.wait_ge(tile_full, n + 1)
                    act.activation(v_ones[:, b, :, :, 0:HD], bank(n).rearrange("p (t h d) -> p t h d", t=T, d=HD), ACT.Copy).then_inc(v_ready, 1)
                elif name in CHUNKS:
                    col = V_B1[layer - 1] if name == "W1" else V_SSM1 if name == "W1S" else V_FF1
                    f = ACT.Gelu if name == "W1S" or (name == "W1" and layer == 1) else ACT.Gelu_apprx_tanh
                    for j in range(CHUNKS[name]):
                        bias = vec[:, V_ZERO:V_ZERO + 1] if col is None else vec[:, col + j:col + j + 1]
                        act.wait_ge(tile_full, n + j + 1)
                        act.activation(hid[:, j, :], bank(n + j), f, bias=bias).then_inc(gelu_done, 1)
                elif name == "SIN":
                    act.wait_ge(ang_ready, 4)
                    act.activation(rot1[:, :, :, :], rot1[:, :, :, :], ACT.Sin).then_inc(sincos, 1)

            act.wait_ge(zeros_set, 1)
            for t in (k_stack, q_stack):
                act.activation(t[:, 1].rearrange("p h s -> p (h s)").bitcast(F32), half[:, 4:5].to_broadcast([P, H * S // 2]), ACT.Copy).then_inc(stack_zero[1], 1)
            act.activation(v_ones[:, 1].rearrange("p t h e -> p (t h e)"), half[:, 4:5].to_broadcast([P, T * H * 32]), ACT.Copy).then_inc(v_set[1], 1)

            for s, i, items in walk():
                if exps_of(s):
                    G, kt = exps_of(s)
                    n = 16 * G + 4 * kt + i
                    act.wait_ge(shifted, n + 1)
                    if n == 0:
                        act.wait_ge(gate_b_ready, 1)
                    if n >= RING_P:
                        act.wait_ge(quad_done, (n - RING_P) // 4 + 1)
                    act.activation(probs[:, n % RING_P, :], exp_ps[:, n % 3, :], ACT.Exp,
                                   scale=SCORE_SCALE[G // GROUPS // NB]).then_inc(exp_done, 1)
                if i == 2 and exps_of(s - LAG_V) and exps_of(s - LAG_V)[1] == T - 1:
                    G = exps_of(s - LAG_V)[0]
                    act.wait_ge(quad_done, 4 * G + 4)
                    if G > 0:
                        act.wait_ge(tile_full, USE[("OG", G - 1, 0)] + 1)
                    act.activation(oT_raw[:, :], pv_ps[:, :], ACT.Copy).then_inc(quad_out, 1)
                for item in items:
                    dense(item)

        @block.vector
        def _(dve):
            steps = [0]

            def settle(ins):
                steps[0] += 1
                ins.then_inc(dve_step, 1)
                dve.wait_ge(dve_step, steps[0])

            def statistics(b, i):
                for t in range(T):
                    ins = dve.bn_stats(bst[:, t, :], x[:, b, t, :])
                settle(ins)
                for t in range(T):
                    ins = dve.bn_aggr(mv[:, i % 2, t, :], bst[:, t, :])
                ins.then_inc(stats_ready, 1)

            def split(k, src, res):
                dve.tensor_copy(parts[:, 1, 0, :], src).then_inc(split_q, 1)
                dve.wait_ge(split_q, 3 * k + 1)
                settle(dve.tensor_tensor(res, src, parts[:, 1, 0, :], ALU.subtract))
                dve.tensor_copy(parts[:, 1, 1, :], res).then_inc(split_q, 1)
                dve.wait_ge(split_q, 3 * k + 2)
                dve.tensor_tensor(parts[:, 1, 2, :], res, parts[:, 1, 1, :], ALU.subtract).then_inc(split_q, 1)

            def dense(item):
                name, k, c = item
                layer, b = chain_of_job_layers(k)
                n = USE[item]
                if name == "ADA0":
                    dve.wait_ge(tile_full, n + 1)
                    settle(dve.tensor_tensor(modv[:, 0:4, :], bank(n)[:, 0:8].rearrange("p (m b) -> p m b", b=NB),
                                             vec[:, V_BIAS:V_BIAS + 4].unsqueeze(2).to_broadcast([P, 4, NB]), ALU.add))
                    dve.tensor_tensor(modv[:, 0:4, :], modv[:, 0:4, :],
                                      vec[:, V_ONE:V_ONE + 4].unsqueeze(2).to_broadcast([P, 4, NB]), ALU.add).then_inc(mod_ready, 1)
                    dve.wait_ge(silu_exp, 1)
                    settle(dve.tensor_scalar(silu[:, 1, :], silu[:, 0, :], 1.0, None, ALU.add))
                    settle(dve.reciprocal(silu[:, 2, :], silu[:, 1, :]))
                    dve.tensor_tensor(silu[:, 3, :], silu[:, 2, :], cond[:, :], ALU.mult).then_inc(cond_ready, 1)
                    dve.tensor_copy(ident_bf[:, :], ident[:, :]).then_inc(cond_ready, 1)
                    dve.wait_ge(cond_ready, 2)
                    dve.tensor_copy(cwide[:, 0:2, :], cond[:, :].unsqueeze(2).to_broadcast([P, NB, P]))
                    dve.tensor_copy(cwide[:, 2:4, :], silu[:, 3, :].unsqueeze(2).to_broadcast([P, NB, P])).then_inc(cond_ready, 1)
                elif name == "ADA1":
                    dve.wait_ge(tile_full, n + 1)
                    settle(dve.tensor_tensor(modv[:, 4:14, :], bank(n)[:, 0:20].rearrange("p (m b) -> p m b", b=NB),
                                             vec[:, V_BIAS + 4:V_BIAS + 14].unsqueeze(2).to_broadcast([P, 10, NB]), ALU.add))
                    dve.tensor_tensor(modv[:, 4:14, :], modv[:, 4:14, :],
                                      vec[:, V_ONE + 4:V_ONE + 14].unsqueeze(2).to_broadcast([P, 10, NB]), ALU.add).then_inc(mod_ready, 1)
                elif name == "GATE":
                    dve.wait_ge(gates_full, 1)
                    dve.wait_ge(rows_in, 16)
                    for r in range(3):
                        ins = dve.tensor_tensor(gate[:, r].rearrange("p g b d -> p g b d"),
                                                exp_ps[:, r, :].rearrange("p (g b d) -> p g b d", g=2, b=NB),
                                                rows[:, 2 * r * D:2 * (r + 1) * D].rearrange("p (g d) -> p g d", g=2).unsqueeze(2).to_broadcast([P, 2, NB, D]),
                                                ALU.add)
                    ins.then_inc(gates_ready, 1)
                elif name == "ST":
                    dve.wait_ge(x_in[k], 16)
                    statistics(b, k)
                elif name == "MK":
                    i = NORM_NO[(k, 1)]
                    dve.wait_ge(late_in, LATE)
                    dve.wait_ge(h_ready, i + 1)
                    if b == 0:
                        settle(dve.tensor_copy(mask_col[:, :, :], mask_u8))
                    dve.tensor_tensor(hT[:, i % 2, :], hT[:, i % 2, :], mask_row[:, b, :], ALU.mult).then_inc(h_masked, 1)
                elif name in ("RK", "RQ"):
                    m = 0 if name == "RK" else 1
                    r = 2 * (k - NB) + m
                    sin = rot1[:, b, 0, :] if layer == 1 else rot2[:, 0, :]
                    dve.wait_ge(tile_full, n + 1)
                    if k == NB:
                        dve.wait_ge(sincos, 1)
                    settle(dve.tensor_tensor(work[:, 4 + m, :], bank(n), sin, ALU.mult))
                    dve.wait_ge(cos_done, r + 1)
                    dve.tensor_tensor(work[:, m, :], work[:, 2 + m, :], work[:, 4 + m, :], ALU.add).then_inc(roped, 1)
                elif name == "SQ":
                    if layer == 0:
                        dve.wait_ge(qk_ready, 2 * k + 2)
                    else:
                        dve.wait_ge(roped, 2 * (k - NB) + 2)
                    if k > 0:
                        dve.wait_ge(stacked_q[(k - 1) % 2], STACK_Q * ((k - 1) // 2 + 1))
                    split(k, work[:, 1, :], work[:, 5, :])
                elif name == "ANG":
                    dve.wait_ge(tile_full, n + 1)
                    dve.tensor_copy(ang[:, :], bank(n)).then_inc(ang_read, 1)
                    dve.wait_ge(ang_read, k + 1)
                elif name == "RED":
                    bb, f = k // 2, k % 2
                    out = rot1[:, bb, f, :]
                    magic = 12582912.0
                    two_pi_hi = 6.28125
                    two_pi_lo = float(2 * np.pi - 6.28125)
                    pi = 3.1415925
                    settle(dve.tensor_scalar(turns[:, :], ang[:, :], float(1 / (2 * np.pi)), 0.25 * f, ALU.mult, ALU.add))
                    settle(dve.tensor_scalar(turns[:, :], turns[:, :], magic, magic, ALU.add, ALU.subtract))
                    settle(dve.scalar_tensor_tensor(out=out, in0=turns[:, :], scalar=-two_pi_hi, in1=ang[:, :], op0=ALU.mult, op1=ALU.add))
                    settle(dve.scalar_tensor_tensor(out=out, in0=turns[:, :], scalar=-two_pi_lo, in1=out, op0=ALU.mult, op1=ALU.add))
                    settle(dve.tensor_scalar(out, out, float(np.pi / 2) * f, pi, ALU.add, ALU.min))
                    ins = dve.tensor_scalar(out, out, -pi, None, ALU.max)
                    ins.then_inc(ang_ready, 1)
                    dve.wait_ge(ang_ready, k + 1)
                elif name == "OG":
                    g = k % GROUPS
                    src = bank(n).rearrange("p (t j e) -> p t j e", t=T, j=4)
                    dve.wait_ge(tile_full, n + 1)
                    if k > 0:
                        dve.wait_ge(o_ready, k)
                    settle(dve.reciprocal(rden[:, :, :], src[:, :, :, HD]))
                    dve.tensor_tensor(o_tok[:, :, 32 * g:32 * g + 32].rearrange("p t (j d) -> p t j d", d=HD), src[:, :, :, 0:HD],
                                      rden[:, :, :].unsqueeze(3).to_broadcast([P, T, 4, HD]), ALU.mult).then_inc(o_ready, 1)
                elif name == "SX":
                    dve.wait_ge(*x_written[k, c])
                    statistics(b, NORM_NO[(k, c)])
                elif name == "XH":
                    i = NORM_NO[(k, c)]
                    dve.wait_ge(rstd_ready, i + 1)
                    for t in range(T):
                        ins = dve.tensor_scalar(xhat[:, i % 2, t, :], x[:, b, t, :], mv[:, i % 2, t, 0:1], rstd[:, i % 2, t:t + 1],
                                                ALU.subtract, ALU.mult)
                    ins.then_inc(xhat_ready, 1)
                elif name == "WO" or name[:2] == "W2":
                    first, tiles = (0, T) if name == "WO" else (c, 1)
                    src = bank(n)[:, 0:tiles * D].rearrange("p (t d) -> p t d", t=tiles)
                    number = residual_no[(name, k, c)]
                    dve.wait_ge(tile_full, n + 1)
                    if (name, k) not in GATED_NO:
                        dve.tensor_tensor(x[:, b, first:first + tiles], src, x[:, b, first:first + tiles], ALU.add).then_inc(res_read, 1)
                        return
                    r, gi = GATE_OF[(name, layer)]
                    g_tile = gate[:, r, gi, b, :].unsqueeze(1).to_broadcast([P, tiles, D])
                    dve.tensor_tensor(gated[:, first:first + tiles, :], src, g_tile, ALU.mult).then_inc(res_read, 1)
                    last = name == "WO" or c == T - 1
                    if first == 0:
                        dve.wait_ge(xg_ready, GATED_NO[(name, k)] + 1)
                    if name == "WO":
                        dve.wait_ge(res_read, number)
                        dve.tensor_tensor(x[:, b], gated[:, :, :], xg[:, b], ALU.add).then_inc(x_ready, 1)
                        return
                    for t in ([c - 1] if c > 0 else []) + ([c] if last else []):
                        dve.wait_ge(res_read, number - c + t)
                        if name == "W2S":
                            ins = dve.scalar_tensor_tensor(out=x[:, b, t, :], in0=gated[:, t, :], scalar=mask_col[:, b, t:t + 1],
                                                           in1=xg[:, b, t, :], op0=ALU.mult, op1=ALU.add)
                        else:
                            ins = dve.tensor_tensor(x[:, b, t, :], gated[:, t, :], xg[:, b, t, :], ALU.add)
                    if last:
                        ins.then_inc(y_ready if name == "W2F" else x_ready, 1)

            zero32 = q_stack[:, 0].rearrange("p h s -> p (h s)").bitcast(F32)
            dve.memset(half[:, 4:5], 0.0).then_inc(zeros_set, 1)
            dve.memset(half[:, 0:T], -0.5).then_inc(id_ready, 1)
            dve.memset(ones_rows[:, :], 1.0).then_inc(ones_tile_set, 1)
            dve.memset(zero32, 0.0).then_inc(stack_zero[0], 1)
            dve.memset(v_ones[:, 0], 0.0).then_inc(v_set[0], 1)
            dve.wait_ge(v_set[0], 1)
            dve.memset(v_ones[:, 0, :, :, HD:HD + 1], 1.0).then_inc(v_set[0], 1)

            for s, i, items in walk():
                if i == 0 and max_rows_of(s) is not None:
                    G = max_rows_of(s)
                    m, r, pt = mx[:, G % 2], mres[:, G % 2], mparts[:, G % 2]
                    dve.wait_ge(*read_of[USE[("max", s - 1, 3)]])
                    settle(dve.tensor_scalar(pt[:, :, 0, :], m, -1.0, None, ALU.mult))
                    settle(dve.tensor_tensor(r, m, pt[:, :, 0, :], ALU.add))
                    settle(dve.tensor_scalar(pt[:, :, 1, :], r, -1.0, None, ALU.mult))
                    settle(dve.tensor_tensor(r, r, pt[:, :, 1, :], ALU.add))
                    dve.tensor_scalar(pt[:, :, 2, :], r, -1.0, None, ALU.mult).then_inc(max_split, 1)
                if maxima_of(s):
                    q, h = maxima_of(s)
                    G, n = GROUPS * q + h // 4, USE[("max", s, i)]
                    dve.wait_ge(tile_full, n + 1)
                    dve.tensor_reduce(mx[:, G % 2, i, h % 4:h % 4 + 1], ring_ps[:, n % TILES, :], AX_X, ALU.max).then_inc(tile_free, 1)
                if i == 2 and max_rows_of(s) is not None:
                    G = max_rows_of(s)
                    n = USE[("rows", s)]
                    dve.wait_ge(tile_full, n + 1)
                    if G >= 2:
                        dve.wait_ge(rows_in_stack[G % 2], 16 * (G // 2))
                    dve.tensor_copy(mrows[:, G % 2, :], ring_ps[0:12, n % TILES, :].bitcast(BF16)[:, 0:S]).then_inc(tile_free, 1)
                for item in items:
                    dense(item)

        @block.gpsimd
        def _(pool):
            steps = [0]

            def settle(ins):
                steps[0] += 1
                ins.then_inc(pool_step, 1)
                pool.wait_ge(pool_step, steps[0])

            def inv_std(i, eps):
                pool.wait_ge(stats_ready, i + 1)
                settle(pool.tensor_scalar(rstd[:, i % 2, :], mv[:, i % 2, :, 1], eps, None, ALU.add))
                pool.tensor_tensor(rstd[:, i % 2, :], rstd[:, i % 2, :], half[:, 0:T], ALU.pow).then_inc(rstd_ready, 1)

            def add_bias(step, k):
                layer, b = chain_of_job_layers(k)
                r, gi = GATE_OF[(step, layer)]
                gb = gate_b[:, r, gi, b, :]
                if step == "W2S":
                    for t in range(T):
                        pool.wait_ge(h_masked, b + 1)
                        ins = pool.tensor_scalar(xg[:, b, t, :], gb, mask_col[:, b, t:t + 1], 1.0, ALU.mult, ALU.mult)
                    settle(ins)
                    pool.tensor_tensor(xg[:, b], xg[:, b], x[:, b], ALU.add).then_inc(xg_ready, 1)
                else:
                    pool.tensor_tensor(xg[:, b], x[:, b], gb.unsqueeze(1).to_broadcast([P, T, D]), ALU.add).then_inc(xg_ready, 1)

            def split(k, src, res):
                pool.tensor_scalar(parts[:, 0, 0, :], src, 1.0, 1.0, ALU.mult, ALU.mult).then_inc(split_k, 1)
                pool.wait_ge(split_k, 3 * k + 1)
                settle(pool.tensor_tensor(res, src, parts[:, 0, 0, :], ALU.subtract))
                pool.tensor_scalar(parts[:, 0, 1, :], res, 1.0, 1.0, ALU.mult, ALU.mult).then_inc(split_k, 1)
                pool.wait_ge(split_k, 3 * k + 2)
                pool.tensor_tensor(parts[:, 0, 2, :], res, parts[:, 0, 1, :], ALU.subtract).then_inc(split_k, 1)

            def dense(item):
                name, k, c = item
                layer, b = chain_of_job_layers(k)
                if name == "ST":
                    if k == 0:
                        pool.wait_ge(id_ready, 1)
                    inv_std(k, EPS[0])
                elif name == "GATE":
                    pool.wait_ge(gates_ready, 1)
                    settle(pool.tensor_tensor(rows[:, 10 * D:11 * D], rows[:, 10 * D:11 * D], rows[:, 11 * D:12 * D], ALU.add))
                    for r in range(3):
                        for gi in range(2):
                            col = (6 + 2 * r + gi) if (r, gi) != (2, 1) else 12
                            ins = pool.tensor_tensor(gate_b[:, r, gi], gate[:, r, gi],
                                                     rows[:, col * D:(col + 1) * D].unsqueeze(1).to_broadcast([P, NB, D]), ALU.mult)
                    ins.then_inc(gate_b_ready, 1)
                elif name == "XG0":
                    pool.wait_ge(gate_b_ready, 1)
                    for bb in range(NB):
                        pool.wait_ge(x_in[bb], 16)
                    add_bias("WO", 2)
                    add_bias("WO", 3)
                    pool.wait_ge(late_in, LATE)
                    pool.tensor_copy(pos_f[:, :, :], pos_i[:, :, :]).then_inc(pos_ready, 1)
                elif name in ("K", "Q") and layer > 0:
                    m = 0 if name == "K" else 1
                    cos = rot1[:, b, 1, :] if layer == 1 else rot2[:, 1, :]
                    if k == NB and m == 0:
                        pool.wait_ge(sincos, 1)
                        pool.wait_ge(late_in, LATE)
                    pool.wait_ge(qk_ready, 2 * k + 1 + m)
                    pool.tensor_tensor(work[:, 2 + m, :], work[:, m, :], cos, ALU.mult).then_inc(cos_done, 1)
                elif name == "RK" or (name == "K" and layer == 0):
                    if layer == 0:
                        pool.wait_ge(qk_ready, 2 * k + 1)
                    else:
                        pool.wait_ge(roped, 2 * (k - NB) + 1)
                    if k > 0:
                        pool.wait_ge(stacked_k[(k - 1) % 2], STACK_K * ((k - 1) // 2 + 1))
                    split(k, work[:, 0, :], work[:, 4, :])
                elif name == "SX":
                    inv_std(NORM_NO[(k, c)], EPS[layer - 1] if c == 0 else EPS[layer])
                    if next_gated(k, c):
                        add_bias(*next_gated(k, c))

            pool.memset(k_stack[:, 0].rearrange("p h s -> p (h s)").bitcast(F32), 0.0).then_inc(stack_zero[0], 1)
            for s, i, items in walk():
                for item in items:
                    dense(item)
                    if item[0] == "ST" and item[1] == 1:
                        pool.wait_ge(v_set[1], 1)
                        pool.memset(v_ones[:, 1, :, :, HD:HD + 1], 1.0).then_inc(v_set[1], 1)


def lay_out(a):
    f = np.float32

    def vecs(*cols):
        return [np.asarray(c, f).reshape(-1, P) for c in cols]

    def heads_inner(m):
        return m.reshape(m.shape[:-1] + (H, HD)).swapaxes(-1, -2).reshape(m.shape)

    def layer(wq, wk, wv, wo, w1, w2):
        return np.concatenate([heads_inner(wq), heads_inner(wk), wv, wo, w1, rows_by_tile(w2)], 1)

    def rows_by_tile(m):
        return m.reshape(-1, P, m.shape[1]).transpose(1, 0, 2).reshape(P, -1)

    b0, b1, b3, b3f = a["L0_cond_b_ada"], a["L1_cond_ada_b"], a["L3_cond_ada_b"], a["L3_cond_ffada_b"]
    zero, one = np.zeros(P, f), np.ones(P, f)
    qkv_w, qkv_b = a["L1_cond_qkv_w"], a["L1_cond_qkv_b"]
    shift_scale = [b[c * D:(c + 1) * D] for b, cs in ((b0, (0, 1, 3, 4)), (b1, (0, 1, 3, 4))) for c in cs]
    shift_scale += [zero, zero] + [b[c * D:(c + 1) * D] for b in (b3, b3f) for c in (0, 1)]
    ones = [one if m % 2 == 1 and m != 9 else zero for m in range(MOD)]
    vec = vecs(*shift_scale, *ones,
               heads_inner(a["L0_cond_bq"]), heads_inner(a["L0_cond_bk"]), a["L0_cond_bv"],
               heads_inner(qkv_b[0:D]), heads_inner(qkv_b[D:2 * D]), qkv_b[2 * D:],
               a["L0_cond_b1"], a["L1_cond_fc1_b"], a["L2_cond_mlp_ln_scale"], a["L3_cond_ssm_b1"], a["L3_cond_bwd_b1"],
               a["L3_cond_ff_b1"])
    vec = np.concatenate(vec, 0)
    pad = np.zeros((V_N - len(vec), P), f)
    vec = np.concatenate([vec, pad], 0).T
    ada = np.concatenate([a["L0_cond_W_ada"], a["L1_cond_ada_w"], a["L2_cond_w_offset"], a["L2_cond_w_scale"],
                          a["L3_cond_ada_w"], a["L3_cond_ffada_w"]], 1)
    gates = [b0[2 * D:3 * D], b0[5 * D:], b1[2 * D:3 * D], b1[5 * D:], b3[2 * D:], b3f[2 * D:]]
    rows = np.concatenate(gates + [a["L0_cond_bo"], a["L0_cond_b2"], a["L1_cond_proj_b"], a["L1_cond_fc2_b"],
                                   a["L3_cond_ssm_b2"], a["L3_cond_bwd_b2"], a["L3_cond_ff_b2"]])[None, :]
    turn = np.zeros((P, 2, P), f)
    freq = np.zeros((2, P), f)
    inv1 = (f(1.0) / f(100.0) ** (np.arange(0, 4, 2, dtype=f) / f(4))).astype(f)
    inv2 = (f(10000.0) ** (-np.arange(0, HD, 2, dtype=f) / f(HD))).astype(f)
    grid = np.arange(S, dtype=f)[:, None] * inv2[None, :]
    rot2 = np.zeros((P, 2, S), f)
    for d in range(HD):
        for h in range(H):
            to = d * H + h
            turn[(d + 2 if d % 4 < 2 else d - 2) * H + h, 0, to] = -1 if d % 4 < 2 else 1
            turn[(d + 1 if d % 2 == 0 else d - 1) * H + h, 1, to] = -1 if d % 2 == 0 else 1
            freq[d // 4, to] = inv1[d % 2]
            rot2[to, 0], rot2[to, 1] = np.sin(grid[:, d // 2].astype(np.float64)), np.cos(grid[:, d // 2].astype(np.float64))
    mask = a["mask_BxS_bk0"].view(np.uint8)
    return {
        "x": a["x"], "cond": a["cond_1024"].T, "vec": vec, "ident": np.eye(P, dtype=f), "ada": ada, "rows": rows,
        "turn": turn, "freq": freq, "rot2": rot2,
        "pos": a["itok_BxSx2_0_63"].transpose(2, 0, 1), "mask_row": mask.view(np.int32),
        "mask_col": np.ascontiguousarray(mask.reshape(NB, T, P).transpose(2, 0, 1)).reshape(P, NB * T).view(np.int32),
        "w0": layer(*[a["L0_cond_" + n] for n in ("Wq", "Wk", "Wv", "Wo", "W1", "W2")]),
        "w1": layer(qkv_w[:, 0:D], qkv_w[:, D:2 * D], qkv_w[:, 2 * D:], a["L1_cond_proj_w"], a["L1_cond_fc1_w"], a["L1_cond_fc2_w"]),
        "w2": layer(*[a["L2_cond_" + n] for n in ("wq", "wk", "wv", "wo", "w1", "w2")]),
        "w3": np.concatenate([a["L3_cond_ssm_w1"], a["L3_cond_bwd_w1"], a["L3_cond_ssm_w2"], a["L3_cond_bwd_w2"],
                              a["L3_cond_ff_w1"], rows_by_tile(a["L3_cond_ff_w2"])], 1),
    }


def kernel(**inputs):
    import concourse.bacc as bacc
    from concourse.bass_utils import run_bass_kernel_spmd

    nc = bacc.Bacc("TRN2", target_bir_lowering=False, num_devices=1)
    arrays, ins = {}, {}
    for name, a in lay_out({n: np.asarray(v) for n, v in inputs.items()}).items():
        a = np.ascontiguousarray(a)
        arrays[f"in_{name}_dram"] = a
        ins[name] = nc.dram_tensor(f"in_{name}_dram", a.shape, mybir.dt.from_np(a.dtype), kind="ExternalInput").ap()
    y = nc.dram_tensor("out_0_dram", (NB, S, D), F32, kind="ExternalOutput").ap()
    build(nc, ins, y)
    r = run_bass_kernel_spmd(nc, [arrays], core_ids=[0])
    return r.results[0]["out_0_dram"]
```

```python
from contextlib import ExitStack

import numpy as np

import concourse.bass as bass
from concourse import mybir

F32 = mybir.dt.float32
BF16 = mybir.dt.bfloat16
I32 = mybir.dt.int32
U8 = mybir.dt.uint8
ALU = mybir.AluOpType
ACT = mybir.ActivationFunctionType
AX_X = mybir.AxisListType.X

P = 128
NB, S, D, H, HD, FF = 2, 512, 128, 16, 8, 512
T = S // P
LAYERS = 3
CHAINS = LAYERS * NB
LAST = CHAINS + NB - 1
GROUPS = H // 4
SCORE_SCALE = [HD ** -0.5, HD ** -0.5, D ** -0.5]
EPS = [1e-5, 1e-6, 1e-5, 1e-6]
PARTS_Q = [0, 0, 0, 1, 1, 2]
PARTS_K = [0, 1, 2, 0, 1, 0]
STACK_K = 16 * len(PARTS_K)
ZERO_ROW = 8 * len(PARTS_K)
MAX_ROW = 96
TILES = 4
RING_P = 12

MOD = 14
V_BIAS, V_ONE, V_BQ, V_BK, V_BV, V_B1, V_LN2, V_SSM1, V_FF1, V_TQ, V_TK, V_ZERO, V_N = 0, 14, [28, 31, 49], [29, 32, 49], [30, 33, 49], [34, 38, None], 42, 43, 45, [None, 47, 49], [None, 48, 49], 49, 50
W_Q, W_K, W_V, W_O, W_1, W_2, W_TQ, W_TK = 0, 128, 256, 384, 512, 1024, 1536, 1664
STRIDE = 17
LAG_B = 6
LAG_V = 1
CLOCK_PRODUCTS = 19
OG_LAG = 4
JOB_LAG = 7
END_LAG = 6
JOB1_AT = 1
ANG_AT = 40
RED_EVERY = 4
SIN_AT = 103
XG0_AT = 29


def chain_of_job_layers(k):
    return k // NB, k % NB


FIRST_JOB = [("ST", 11), ("XH", 7), ("TR", 5), ("K", 2), ("Q", 1), ("SQ", 0), ("DK", 0), ("DK", 6), ("DK", 0), ("DQ", 0),
             ("DQ", 1), ("DQ", 1), ("V", 1)]
MID_JOB = [("OT", 4), ("WO", 0), ("SX", 3), ("XH", 3), ("TR", 3), ("W1", 0), ("W2", 1), ("SX", 3), ("XH", 2), ("TR", 1),
           ("K", 0), ("Q", 1), ("RK", 3), ("RQ", 7), ("SQ", 1), ("DK", 0), ("DK", 0), ("DK", 4), ("DQ", 0), ("DQ", 0),
           ("DQ", 1), ("V", 1)]
LAST_JOB = [("OT", 3), ("WO", 0), ("SX", 4), ("XH", 4), ("TR", 25), ("W1", 0), ("W2", 6), ("SX", 1), ("XH", 1), ("TR", 1),
            ("MK", 7), ("W1S", 3), ("W2S", 0), ("SX", 0), ("XH", 11), ("TR", 0), ("W1F", 3), ("W2F", 20)]
END_JOB = [("OT", 3), ("WO", 3), ("SX", 7), ("XH", 3), ("TR", 0), ("W1", 0), ("W2", 4), ("SX", 0), ("XH", 0), ("TR", 6),
           ("MK", 10), ("W1S", 0), ("W2S", 1), ("SX", 2), ("XH", 12), ("TR", 0), ("W1F", 0), ("W2F", 8)]
CHUNKS = {"W1": 4, "W1S": 2, "W1F": 2}


def steps_of_job(k):
    return FIRST_JOB if k < NB else MID_JOB if k < CHAINS else LAST_JOB if k < LAST else END_JOB


def make_plan():
    last = STRIDE * (CHAINS - 1) + LAG_B + H + LAG_V + 1
    plan = [[[] for _ in range(4)] for _ in range(last + 60)]

    def put(at, item):
        plan[at // 4][at % 4].append(item)

    def put_job(k, at):
        for name, gap in steps_of_job(k):
            put(at, (name, k))
            at += gap
        return at

    plan[0][0] = [(name, 0) for name, _ in FIRST_JOB] + [("ADA1", 0), ("GATE", 0)]
    plan[0][0].insert(2, ("ADA0", 0))
    end = put_job(1, JOB1_AT)
    put(XG0_AT, ("XG0", 0))
    at = ANG_AT
    for b in range(NB):
        put(at, ("ANG", b))
        for f in range(2):
            put(at + 1 + RED_EVERY * f, ("RED", 2 * b + f))
        at += 2 * RED_EVERY
    put(SIN_AT, ("SIN", 0))
    for q in range(CHAINS):
        for g in range(GROUPS):
            put(4 * (first_slot(q) + LAG_B + 4 * g + 3 + LAG_V) + OG_LAG, ("OG", GROUPS * q + g))
        k = q + NB
        start = 4 * (first_slot(q) + LAG_B + H - 1 + LAG_V) + (END_LAG if k == LAST else JOB_LAG)
        end = put_job(k, start if k == LAST else max(start, end))
    used = max(s for s, sl in enumerate(plan) if any(sl))
    return plan[:used + 1]


def first_slot(q):
    return 1 + STRIDE * q


PLAN = make_plan()
SLOTS = len(PLAN)


def maxima_of(s):
    for q in range(CHAINS):
        if 0 <= s - first_slot(q) < H:
            return q, s - first_slot(q)
    return None


def exps_of(s):
    for q in range(CHAINS):
        n = s - first_slot(q) - LAG_B
        if 0 <= n < H:
            return GROUPS * q + n // 4, n % 4
    return None


def max_rows_of(s):
    for q in range(CHAINS):
        n = s - first_slot(q)
        if n in (4, 8, 12, 16):
            return GROUPS * q + n // 4 - 1
    return None


def banks_of(name):
    if name in CHUNKS:
        return CHUNKS[name]
    if name[:2] == "W2":
        return T
    return int(name in ("ADA0", "ADA1", "OG", "OT", "WO", "TR", "K", "Q", "V", "RK", "RQ", "ANG"))


def number_uses():
    use, seen, maxima, rows, n = {}, {}, [], [], 0
    for s in range(SLOTS):
        for i in range(4):
            if maxima_of(s):
                use[("max", s, i)] = n
                maxima.append(n)
                n += 1
            if i == 2 and max_rows_of(s) is not None:
                use[("rows", s)] = n
                rows.append(n)
                n += 1
            for item in PLAN[s][i]:
                c = seen.get(item, 0)
                seen[item] = c + 1
                use[item + (c,)] = n
                n += banks_of(item[0])
    return use, maxima, rows


USE, MAXIMA_USES, ROWS_USES = number_uses()


def walk():
    seen = {}
    for s in range(SLOTS):
        for i in range(4):
            items = []
            for item in PLAN[s][i]:
                n = seen.get(item, 0)
                seen[item] = n + 1
                items.append((item[0], item[1], n))
            yield s, i, items


def next_gated(k, c):
    layer = k // NB
    return {(1, 0): ("W2", k), (1, 1): ("WO", k + NB), (2, 0): ("W2", k), (3, 1): ("W2S", k), (3, 2): ("W2F", k)}.get((layer, c))


def norm_order():
    norm_no, n = {}, 0
    gated_no, g = {}, 0
    for _, _, items in walk():
        for name, k, c in items:
            if name in ("ST", "SX"):
                norm_no[(k, c)] = n
                n += 1
            if name == "XG0":
                gated_no[("WO", 2)], gated_no[("WO", 3)] = g, g + 1
                g += 2
            layer = k // NB
            nxt = next_gated(k, c) if name == "SX" else None
            if nxt:
                gated_no[nxt] = g
                g += 1
    return norm_no, gated_no


NORM_NO, GATED_NO = norm_order()


def check_plan():
    at, n = {}, 0
    for _, _, items in walk():
        for item in items:
            n += 1
            at[item] = n
    for (name, k, c), here in at.items():
        job_norm = {"K": 0, "Q": 0, "RK": 0, "RQ": 0, "V": 0, "MK": 1, "W1": 0, "W1S": 1, "W1F": 2}.get(name)
        if job_norm is not None:
            if name in ("K", "Q", "RK", "RQ", "V") and k >= NB:
                job_norm = 1
            later = [key for key, i in NORM_NO.items() if i == NORM_NO[k, job_norm] + 2]
            assert all(here < at["TR", key[0], key[1]] for key in later), (name, k)
        if name == "TR":
            later = [key for key, i in NORM_NO.items() if i == NORM_NO[k, c] + 2]
            assert all(here < at["XH", key[0], key[1]] for key in later), (name, k)
        if name == "XH":
            later = [key for key, i in NORM_NO.items() if i == NORM_NO[k, c] + 2]
            assert all(here < at["SX" if key[0] >= NB else "ST", key[0], key[1]] for key in later), (name, k)
        if name in CHUNKS:
            assert not any(here < p < at["W2" + name[2:], k, 0] for (m, _, _), p in at.items() if m in CHUNKS), (name, k)
        if name == "OT" and k < LAST:
            assert here < at["OG", GROUPS * (k - NB + 1), 0] and at["WO", k, 0] < at["OT", k + 1, 0]


check_plan()
GATE_OF = {("WO", 1): (0, 0), ("W2", 1): (0, 1), ("WO", 2): (1, 0), ("W2", 2): (1, 1), ("W2S", 3): (2, 0), ("W2F", 3): (2, 1)}


def build(nc, ins, y):
    ctx = ExitStack()
    with ctx:
        def sb(name, shape, dt=F32):
            return ctx.enter_context(nc.sbuf_tensor(name, shape, dt))

        def sem(name):
            return ctx.enter_context(nc.semaphore(name))

        x = sb("x", [P, NB, T, D])
        xg = sb("xg", [P, NB, T, D])
        q_stack = sb("q_stack", [P, NB, H, S], BF16)
        k_stack = sb("k_stack", [P, NB, H, S], BF16)
        v_ones = sb("v_ones", [P, NB, T, H, 32])
        probs = sb("probs", [P, RING_P, S])
        w = [sb(f"w{n}", [P, (1536, 1792, 1792, 1024)[n]]) for n in range(LAYERS + 1)]
        vec = sb("vec", [P, V_N])
        modv = sb("modv", [P, MOD, NB])
        gate = sb("gate", [P, 3, 2, NB, D])
        gate_b = sb("gate_b", [P, 3, 2, NB, D])
        ident = sb("ident", [P, P])
        ident_bf = sb("ident_bf", [P, P], BF16)
        freq = sb("freq", [2, P])
        pos_i = sb("pos_i", [2, NB, S], I32)
        pos_f = sb("pos_f", [2, NB, S])
        rot1 = sb("rot1", [P, NB, 2, S])
        rot2 = sb("rot2", [P, 2, S])
        mask_words = sb("mask_words", [P, NB, S // 4], I32)
        mask_row = mask_words[:, :, :].bitcast(U8)
        mask_col_words = sb("mask_col_words", [P, NB * T // 4], I32)
        mask_u8 = mask_col_words[:, :].bitcast(U8).rearrange("p (b t) -> p b t", b=NB)
        mask_col = sb("mask_col", [P, NB, T])
        cond = sb("cond", [P, NB])
        silu = sb("silu", [P, 4, NB])
        xhat = sb("xhat", [P, 2, T, D])
        hT = sb("hT", [P, 2, S])
        work = sb("work", [P, 6, S])
        hid = work[:, 0:4]
        parts = sb("parts", [P, 2, 3, S], BF16)
        oT_raw = sb("oT_raw", [P, S])
        o_tok = sb("o_tok", [P, T, D])
        oT = sb("oT", [P, S])
        rden = sb("rden", [P, T, 4])
        gated = work[:, 5].rearrange("p (t d) -> p t d", t=T)
        table_try = sb("table_try", [P, 1])
        bst = sb("bst", [P, NB, T, 6])
        mv = sb("mv", [P, 2, T, 2])
        var_eps = sb("var_eps", [P, 2, T])
        rstd = sb("rstd", [P, 2, T])
        half = sb("half", [P, 5])
        mx = sb("mx", [P, 2, T, 4])
        mres = sb("mres", [P, 2, T, 4])
        mparts = sb("mparts", [P, 2, T, 3, 4], BF16)
        ones_rows = sb("ones_rows", [3, S], BF16)
        mrows = sb("mrows", [12, 2, S], BF16)
        ang, turns = work[:, 2:4], work[:, 4]
        pflat = probs[:, :, :].rearrange("p a b -> p (a b)")
        ada = pflat[:, 0:2560]
        rows = pflat[:, 2560:2560 + 13 * D]
        cwide = pflat[:, 4608:4608 + 4 * P].rearrange("p (a n) -> p a n", a=4)

        ring_ps = ctx.enter_context(nc.psum_tensor("ring_ps", [P, TILES, S], F32))
        exp_ps = ctx.enter_context(nc.psum_tensor("exp_ps", [P, 3, S], F32))
        pv_ps = ctx.enter_context(nc.psum_tensor("pv_ps", [P, S], F32))

        x_in = [sem(f"x{b}_in") for b in range(NB)]
        small_in, ada0_in, ada1_in, rows_in = sem("small_in"), sem("ada0_in"), sem("ada1_in"), sem("rows_in")
        w_in = [sem(f"w{n}_in") for n in range(LAYERS + 1)]
        late_in = sem("late_in")
        k_zero = [sem(f"k_zero{b}") for b in range(NB)]
        q_zero = [sem(f"q_zero{b}") for b in range(NB)]
        v_set = [sem(f"v_set{b}") for b in range(NB)]
        zeros_set, ones_tile_set = sem("zeros_set"), sem("ones_tile_set")
        ones_set = [sem(f"ones_set{b}") for b in range(NB)]
        stacked_k = [sem(f"stacked_k{b}") for b in range(NB)]
        stacked_q = [sem(f"stacked_q{b}") for b in range(NB)]
        tile_full, tile_free = sem("tile_full"), sem("tile_free")
        max_split = sem("max_split")
        rows_out = sem("rows_out")
        rows_in_stack = [sem(f"rows_in_stack{n}") for n in range(2)]
        shifted, exp_done, quad_done, quad_out = sem("shifted"), sem("exp_done"), sem("quad_done"), sem("quad_out")
        v_ready, o_ready = sem("v_ready"), sem("o_ready")
        gelu_done = sem("gelu_done")
        x_ready = sem("x_ready")
        res_read, ang_read = sem("res_read"), sem("ang_read")
        cond_ready, silu_exp, mod_ready = sem("cond_ready"), sem("silu_exp"), sem("mod_ready")
        gates_full, gates_ready, gate_b_ready = sem("gates_full"), sem("gates_ready"), sem("gate_b_ready")
        id_ready, pos_ready, ang_ready, sincos = sem("id_ready"), sem("pos_ready"), sem("ang_ready"), sem("sincos")
        stats_ready, rstd_ready, xhat_ready, h_ready, h_masked = sem("stats_ready"), sem("rstd_ready"), sem("xhat_ready"), sem("h_ready"), sem("h_masked")
        qk_ready, cos_done, roped, split_k, split_q = sem("qk_ready"), sem("cos_done"), sem("roped"), sem("split_k"), sem("split_q")
        oT_ready, xg_ready, y_ready, y_out = sem("oT_ready"), sem("xg_ready"), sem("y_ready"), sem("y_out")
        dve_step, pool_step = sem("dve_step"), sem("pool_step")

        def bank(n):
            return ring_ps[:, n % TILES, :]

        def mlp_weights(name, layer):
            if name in ("W1", "W2"):
                t = w[layer - 1]
                return t[:, W_1:W_1 + FF], t[:, W_2:W_2 + FF]
            t = w[LAYERS]
            return (t[:, 0:256], t[:, 256:512]) if name in ("W1S", "W2S") else (t[:, 512:768], t[:, 768:1024])

        def norm_of(name, k):
            layer = k // NB
            if layer == 0:
                return NORM_NO[(k, 0)]
            if name == "W1":
                return NORM_NO[(k, 0)]
            if name == "W1F":
                return NORM_NO[(k, 2)]
            return NORM_NO[(k, 1)]

        read_of = {n: (tile_free, m + 1) for m, n in enumerate(MAXIMA_USES)}
        read_of.update({n: (rows_out, m + 1) for m, n in enumerate(ROWS_USES)})
        gelu_no, residual_no, x_written = {}, {}, {}
        gelus = residuals = written = 0
        for _, _, items in walk():
            for name, k, c in items:
                n = USE[(name, k, c)]
                if name in CHUNKS:
                    for j in range(CHUNKS[name]):
                        gelus += 1
                        gelu_no[(name, k, j)] = gelus
                        read_of[n + j] = (gelu_done, gelus)
                elif name == "WO" or name[:2] == "W2":
                    for t in range(banks_of(name)):
                        residuals += 1
                        residual_no[(name, k, t)] = residuals
                        read_of[n + t] = (res_read, residuals)
                        gated_step = (name, k) in GATED_NO
                        written += gated_step and name != "W2F"
                        x_written[name, k, t] = (x_ready, written) if gated_step else (res_read, residuals)
                elif banks_of(name):
                    read_of[n] = {
                        "ADA0": (mod_ready, 1), "ADA1": (mod_ready, 2), "V": (v_ready, k + 1), "OG": (o_ready, k + 1),
                        "TR": (h_ready, NORM_NO.get((k, c), 0) + 1), "K": (qk_ready, 2 * k + 1), "Q": (qk_ready, 2 * k + 2),
                        "OT": (oT_ready, k - NB + 1), "ANG": (ang_read, k + 1),
                        "RK": (roped, 2 * (k - NB) + 1), "RQ": (roped, 2 * (k - NB) + 2),
                    }[name]

        block = ctx.enter_context(nc.Block())

        @block.sync
        def _(sp):
            sp.dma_start(x[:, 0], ins["x"][0].rearrange("(t p) d -> p t d", p=P)).then_inc(x_in[0], 16)
            sp.dma_start(cond[:, :], ins["cond"]).then_inc(small_in, 16)
            sp.dma_start(vec[:, :], ins["vec"]).then_inc(small_in, 16)
            sp.dma_start(ident[:, :], ins["ident"]).then_inc(small_in, 16)
            sp.dma_start(ada[:, 0:768], ins["ada"][:, 0:768]).then_inc(ada0_in, 16)
            sp.dma_start(w[0][:, 0:512], ins["w0"][:, 0:512]).then_inc(w_in[0], 16)
            sp.dma_start(x[:, 1], ins["x"][1].rearrange("(t p) d -> p t d", p=P)).then_inc(x_in[1], 16)
            sp.dma_start(ada[:, 768:2560], ins["ada"][:, 768:2560]).then_inc(ada1_in, 16)
            sp.dma_start(rows, ins["rows"].to_broadcast([P, 13 * D])).then_inc(rows_in, 16)

            def stack(k, which, part, target, of_part, split_done, done):
                layer, b = chain_of_job_layers(k)
                sp.wait_ge(split_done, 3 * k + part + 1)
                for r in range(len(of_part)):
                    if of_part[r] == part:
                        sp.dma_start(target[8 * r:8 * r + 8, b], parts[:, which, part, :]).then_inc(done[b], 16)

            for s, i, items in walk():
                if i == 3 and max_rows_of(s) is not None:
                    G = max_rows_of(s)
                    b = (G // GROUPS) % NB
                    sp.wait_ge(*read_of[USE[("rows", s)]])
                    sp.dma_start(q_stack[MAX_ROW:MAX_ROW + 3, b, 4 * (G % GROUPS):4 * (G % GROUPS) + 4, :],
                                 mrows[:, G % 2, :]).then_inc(rows_in_stack[G % 2], 16)
                for name, k, c in items:
                    if name == "DK":
                        if k < NB and c == 0:
                            sp.wait_ge(k_zero[k], 1)
                            sp.wait_ge(ones_tile_set, 1)
                            sp.dma_start(k_stack[MAX_ROW:MAX_ROW + 3, k], ones_rows[:, :].unsqueeze(1).to_broadcast([3, H, S])).then_inc(ones_set[k], 16)
                        stack(k, 0, c, k_stack, PARTS_K, split_k, stacked_k)
                    if name == "DQ":
                        b = k % NB
                        if c == 0 and k < NB:
                            sp.wait_ge(q_zero[k], 1)
                        elif c == 0:
                            sp.dma_start(q_stack[MAX_ROW:MAX_ROW + 3, b], k_stack[ZERO_ROW:ZERO_ROW + 3, b]).then_inc(stacked_q[b], 16)
                        stack(k, 1, c, q_stack, PARTS_Q, split_q, stacked_q)
                        if k == 0 and c == 2:
                            sp.dma_start(w[0][:, 512:1536], ins["w0"][:, 512:1536]).then_inc(w_in[0], 16)
                            sp.dma_start(freq[:, :], ins["freq"]).then_inc(late_in, 16)
                            sp.dma_start(pos_i[:, :, :], ins["pos"]).then_inc(late_in, 16)
                            sp.dma_start(rot2[:, :, :], ins["rot2"]).then_inc(late_in, 16)
                            for b in range(NB):
                                sp.dma_start(mask_words[:, b, :], ins["mask_row"][b:b + 1, :].to_broadcast([P, S // 4])).then_inc(late_in, 16)
                            sp.dma_start(mask_col_words[:, :], ins["mask_col"]).then_inc(late_in, 16)
                            for n in range(1, LAYERS + 1):
                                sp.dma_start(w[n][:, :], ins[f"w{n}"]).then_inc(w_in[n], 16)
            for b in range(NB):
                sp.wait_ge(y_ready, b + 1)
                sp.dma_start(y[b].rearrange("(t p) d -> p t d", p=P), x[:, b]).then_inc(y_out, 16)
            sp.wait_ge(y_out, 16 * NB)
        LATE = 16 * 6

        def q_rows_copied(k):
            return 16 * len(PARTS_Q) * (k // NB + 1) + 16 * (k // NB)


        @block.tensor
        def _(pe):
            def take(n):
                if n >= TILES:
                    pe.wait_ge(*read_of[n - TILES])

            def turn_tiles(n, src, ready=None):
                for t in range(T):
                    if ready:
                        pe.wait_ge(ready[0], ready[1] + t)
                    mm = pe.transpose(bank(n)[:, t * P:(t + 1) * P], src(t), ident[:, :])
                mm.then_inc(tile_full, 1)

            def keep_clock_up(products):
                for _ in range(products):
                    pe.matmul(exp_ps[:, 0, :], k_stack[:, 0, 0, 0:P], q_stack[:, 0, 0, :], start=True, stop=True)

            def token_product(n, lhs, weights):
                for t in range(T):
                    mm = pe.matmul(bank(n)[:, t * D:(t + 1) * D], lhs[:, t * P:(t + 1) * P], weights, start=True, stop=True)
                mm.then_inc(tile_full, 1)

            def dense(item):
                name, k, c = item
                layer, b = chain_of_job_layers(k)
                n = USE[item]
                if name == "ADA0":
                    pe.wait_ge(small_in, 48)
                    pe.wait_ge(ada0_in, 16)
                    take(n)
                    for m, col in enumerate((0, 1, 3, 4)):
                        mm = pe.matmul(bank(n)[:, 2 * m:2 * m + 2], ada[:, col * D:(col + 1) * D], cond[:, :], start=True, stop=True)
                    mm.then_inc(tile_full, 1)
                elif name == "ADA1":
                    pe.wait_ge(ada1_in, 16)
                    pe.wait_ge(cond_ready, 2)
                    take(n)
                    cols = [(6, 1), (7, 1), (9, 1), (10, 1), (12, 0), (13, 0), (14, 1), (15, 1), (17, 1), (18, 1)]
                    for m, (col, act) in enumerate(cols):
                        rhs = silu[:, 3, :] if act else cond[:, :]
                        mm = pe.matmul(bank(n)[:, 2 * m:2 * m + 2], ada[:, col * D:(col + 1) * D], rhs, start=True, stop=True)
                    mm.then_inc(tile_full, 1)
                elif name == "GATE":
                    pe.wait_ge(cond_ready, 3)
                    for r, (cols, act) in enumerate((((2, 5), 0), ((8, 11), 1), ((16, 19), 1))):
                        for g, col in enumerate(cols):
                            for bb in range(NB):
                                o = (2 * g + bb) * D
                                mm = pe.matmul(exp_ps[:, r, o:o + D], cwide[:, 2 * act + bb, :], ada[:, col * D:(col + 1) * D], start=True, stop=True)
                    mm.then_inc(gates_full, 1)
                elif name == "TR":
                    i = NORM_NO[(k, c)]
                    take(n)
                    turn_tiles(n, lambda t: xhat[:, i % 2, t, :], (xhat_ready, T * i + 1))
                elif name in ("K", "Q"):
                    i = norm_of(name, k)
                    pe.wait_ge(h_ready, i + 1)
                    pe.wait_ge(w_in[layer], 16)
                    take(n)
                    o = W_K if name == "K" else W_Q
                    pe.matmul(bank(n), w[layer][:, o:o + D], hT[:, i % 2, :], start=True, stop=True).then_inc(tile_full, 1)
                elif name == "V":
                    i = norm_of(name, k)
                    pe.wait_ge(h_ready, i + 1)
                    take(n)
                    token_product(n, hT[:, i % 2, :], w[layer][:, W_V:W_V + D])
                elif name in ("RK", "RQ"):
                    i = norm_of(name, k)
                    o = W_TK if name == "RK" else W_TQ
                    pe.wait_ge(h_ready, i + 1)
                    pe.wait_ge(w_in[layer], 16)
                    take(n)
                    pe.matmul(bank(n), w[layer][:, o:o + D], hT[:, i % 2, :], start=True, stop=True).then_inc(tile_full, 1)
                elif name == "ANG":
                    pe.wait_ge(pos_ready, 1)
                    take(n)
                    pe.matmul(bank(n), freq[:, :], pos_f[:, k, :], start=True, stop=True).then_inc(tile_full, 1)
                elif name == "OG":
                    pe.wait_ge(quad_out, k + 1)
                    take(n)
                    turn_tiles(n, lambda t: oT_raw[:, t * P:(t + 1) * P])
                elif name == "OT":
                    q = k - NB
                    pe.wait_ge(o_ready, GROUPS * (q + 1))
                    take(n)
                    turn_tiles(n, lambda t: o_tok[:, t, :])
                elif name == "WO":
                    pe.wait_ge(oT_ready, k - NB + 1)
                    take(n)
                    token_product(n, oT, w[layer - 1][:, W_O:W_O + D])
                    if k == LAST:
                        pe.wait_ge(exp_done, 16 * GROUPS * CHAINS)
                        keep_clock_up(CLOCK_PRODUCTS)
                elif name in CHUNKS:
                    i = norm_of(name, k)
                    if name == "W1S":
                        pe.wait_ge(h_masked, b + 1)
                    else:
                        pe.wait_ge(h_ready, i + 1)
                    if name == "W1":
                        pe.wait_ge(w_in[layer - 1], 32 if layer == 1 else 16)
                    else:
                        pe.wait_ge(w_in[LAYERS], 16)
                    w1, _ = mlp_weights(name, layer)
                    for j in range(CHUNKS[name]):
                        take(n + j)
                        pe.matmul(bank(n + j), w1[:, j * P:(j + 1) * P], hT[:, i % 2, :], start=True, stop=True).then_inc(tile_full, 1)
                elif name[:2] == "W2":
                    chunks = CHUNKS["W1" + name[2:]]
                    _, w2 = mlp_weights(name, layer)
                    for j in range(chunks):
                        pe.wait_ge(gelu_done, gelu_no["W1" + name[2:], k, j])
                        for t in range(T):
                            if j == 0:
                                take(n + t)
                            mm = pe.matmul(bank(n + t)[:, 0:D], hid[:, j, t * P:(t + 1) * P], w2[:, j * D:(j + 1) * D],
                                           start=(j == 0), stop=(j == chunks - 1))
                            if j == chunks - 1:
                                mm.then_inc(tile_full, 1)
                    if k == LAST and name != "W2F":
                        keep_clock_up(CLOCK_PRODUCTS)

            for s, i, items in walk():
                if exps_of(s):
                    G, kt = exps_of(s)
                    q, g = G // GROUPS, G % GROUPS
                    b, h, n = q % NB, 4 * g + i, 16 * G + 4 * kt + i
                    if kt == 0 and i == 0:
                        pe.wait_ge(rows_in_stack[G % 2], 16 * (G // 2 + 1))
                        if G == 0:
                            pe.wait_ge(gates_ready, 1)
                    if n >= 3:
                        pe.wait_ge(exp_done, n - 2)
                    pe.matmul(exp_ps[:, n % 3, :], k_stack[:, b, h, kt * P:(kt + 1) * P], q_stack[:, b, h, :],
                              start=True, stop=True).then_inc(shifted, 1)
                if maxima_of(s):
                    q, h = maxima_of(s)
                    b, n = q % NB, USE[("max", s, i)]
                    if h == 0 and i == 0:
                        if q < NB:
                            pe.wait_ge(ones_set[b], 16)
                        pe.wait_ge(stacked_k[b], STACK_K * (q // NB + 1))
                        pe.wait_ge(stacked_q[b], q_rows_copied(q))
                    take(n)
                    pe.matmul(ring_ps[:, n % TILES, :], q_stack[:, b, h, i * P:(i + 1) * P], k_stack[:, b, h, :],
                              start=True, stop=True).then_inc(tile_full, 1)
                if i == 1 and exps_of(s - LAG_V):
                    G, kt = exps_of(s - LAG_V)
                    q, g = G // GROUPS, G % GROUPS
                    b = q % NB
                    pe.wait_ge(exp_done, 16 * G + 4 * kt + 4)
                    if kt == 0:
                        pe.wait_ge(v_ready, q + 1)
                        if G > 0:
                            pe.wait_ge(quad_out, G)
                    for j in range(4):
                        n = 16 * G + 4 * kt + j
                        mm = pe.matmul(pv_ps[32 * j:32 * j + 32, :], v_ones[:, b, kt, 4 * g + j, :], probs[:, n % RING_P, :],
                                       start=(kt == 0), stop=(kt == T - 1))
                    mm.then_inc(quad_done, 1)
                if i == 2 and max_rows_of(s) is not None:
                    G = max_rows_of(s)
                    n = USE[("rows", s)]
                    pe.wait_ge(max_split, G + 1)
                    take(n)
                    out = ring_ps[:, n % TILES, :].bitcast(BF16)
                    for t in range(T):
                        mm = pe.transpose(out[0:12, t * P:(t + 1) * P], mparts[:, G % 2, t].rearrange("p a b -> p (a b)"), ident_bf[:, :])
                    mm.then_inc(tile_full, 1)
                for item in items:
                    dense(item)

        @block.scalar
        def _(act):
            def bring_table(f):
                act.activation(table_try[:, :], half[:, 4:5], f)

            def dense(item):
                name, k, c = item
                layer, b = chain_of_job_layers(k)
                n = USE[item]
                if name == "ADA0":
                    act.wait_ge(small_in, 48)
                    act.activation(silu[:, 0, :], cond[:, :], ACT.Exp, scale=-1.0).then_inc(silu_exp, 1)
                elif name == "TR":
                    i = NORM_NO[(k, c)]
                    if layer == 0:
                        act.wait_ge(mod_ready, 1)
                        sh, sc = modv[:, 0, b:b + 1], modv[:, 1, b:b + 1]
                    else:
                        act.wait_ge(mod_ready, 2)
                        cols = {(1, 0): 2, (1, 1): 4, (2, 0): 6, (2, 1): 8, (3, 1): 10, (3, 2): 12}.get((layer, c))
                        if cols is None:
                            sh, sc = vec[:, V_ZERO:V_ZERO + 1], vec[:, V_LN2:V_LN2 + 1]
                        else:
                            sh, sc = modv[:, cols, b:b + 1], modv[:, cols + 1, b:b + 1]
                    act.wait_ge(tile_full, n + 1)
                    act.activation(hT[:, i % 2, :], bank(n), ACT.Identity, bias=sh, scale=sc).then_inc(h_ready, 1)
                elif name in ("K", "Q"):
                    col = (V_BK if name == "K" else V_BQ)[layer]
                    act.wait_ge(tile_full, n + 1)
                    act.activation(work[:, 0 if name == "K" else 1, :], bank(n), ACT.Identity, bias=vec[:, col:col + 1]).then_inc(qk_ready, 1)
                elif name == "OT":
                    col = V_BV[layer - 1]
                    act.wait_ge(tile_full, n + 1)
                    act.activation(oT[:, :], bank(n), ACT.Identity, bias=vec[:, col:col + 1]).then_inc(oT_ready, 1)
                    if k == LAST:
                        bring_table(ACT.Gelu_apprx_tanh)
                elif name == "V":
                    if k < NB:
                        act.wait_ge(v_set[k], 2)
                    act.wait_ge(tile_full, n + 1)
                    act.activation(v_ones[:, b, :, :, 0:HD], bank(n).rearrange("p (t h d) -> p t h d", t=T, d=HD), ACT.Copy).then_inc(v_ready, 1)
                    if k == 0:
                        act.wait_ge(zeros_set, 1)
                        for t, done in ((v_ones[:, 1].rearrange("p t h e -> p (t h e)"), v_set[1]),
                                        (k_stack[:, 1].rearrange("p h s -> p (h s)").bitcast(F32), k_zero[1]),
                                        (q_stack[:, 1].rearrange("p h s -> p (h s)").bitcast(F32), q_zero[1])):
                            act.activation(t, half[:, 4:5].to_broadcast([P, t.shape[1]]), ACT.Copy).then_inc(done, 1)
                elif name in CHUNKS:
                    col = V_B1[layer - 1] if name == "W1" else V_SSM1 if name == "W1S" else V_FF1
                    f = ACT.Gelu if name == "W1S" or (name == "W1" and layer == 1) else ACT.Gelu_apprx_tanh
                    for j in range(CHUNKS[name]):
                        bias = vec[:, V_ZERO:V_ZERO + 1] if col is None else vec[:, col + j:col + j + 1]
                        act.wait_ge(tile_full, n + j + 1)
                        act.activation(hid[:, j, :], bank(n + j), f, bias=bias).then_inc(gelu_done, 1)
                    if k == LAST and name != "W1F":
                        bring_table(ACT.Gelu if name == "W1" else ACT.Gelu_apprx_tanh)
                elif name == "ANG":
                    act.wait_ge(tile_full, n + 1)
                    act.activation(ang[:, k, :], bank(n), ACT.Copy).then_inc(ang_read, 1)
                elif name == "SIN":
                    act.wait_ge(ang_ready, 4)
                    act.activation(rot1[:, :, :, :], rot1[:, :, :, :], ACT.Sin).then_inc(sincos, 1)

            for s, i, items in walk():
                if exps_of(s):
                    G, kt = exps_of(s)
                    n = 16 * G + 4 * kt + i
                    act.wait_ge(shifted, n + 1)
                    if n == 0:
                        act.wait_ge(gate_b_ready, 1)
                    if n >= RING_P:
                        act.wait_ge(quad_done, (n - RING_P) // 4 + 1)
                    act.activation(probs[:, n % RING_P, :], exp_ps[:, n % 3, :], ACT.Exp,
                                   scale=SCORE_SCALE[G // GROUPS // NB]).then_inc(exp_done, 1)
                if i == 2 and exps_of(s - LAG_V) and exps_of(s - LAG_V)[1] == T - 1:
                    G = exps_of(s - LAG_V)[0]
                    act.wait_ge(quad_done, 4 * G + 4)
                    if G > 0:
                        act.wait_ge(tile_full, USE[("OG", G - 1, 0)] + 1)
                    act.activation(oT_raw[:, :], pv_ps[:, :], ACT.Copy).then_inc(quad_out, 1)
                if i == 2 and max_rows_of(s) is not None:
                    G = max_rows_of(s)
                    n = USE[("rows", s)]
                    act.wait_ge(tile_full, n + 1)
                    if G >= 2:
                        act.wait_ge(rows_in_stack[G % 2], 16 * (G // 2))
                    act.activation(mrows[:, G % 2, :], bank(n)[0:12].bitcast(BF16)[:, 0:S], ACT.Copy).then_inc(rows_out, 1)
                for item in items:
                    dense(item)

        @block.vector
        def _(dve):
            steps = [0]

            def settle(ins):
                steps[0] += 1
                ins.then_inc(dve_step, 1)
                dve.wait_ge(dve_step, steps[0])

            def statistics(b, i, eps):
                for t in range(T):
                    ins = dve.bn_aggr(mv[:, i % 2, t, :], bst[:, b, t, :])
                settle(ins)
                dve.tensor_scalar(var_eps[:, i % 2, :], mv[:, i % 2, :, 1], eps, None, ALU.add).then_inc(stats_ready, 1)

            def split(k, src, res):
                dve.tensor_copy(parts[:, 1, 0, :], src).then_inc(split_q, 1)
                dve.wait_ge(split_q, 3 * k + 1)
                settle(dve.tensor_tensor(res, src, parts[:, 1, 0, :], ALU.subtract))
                dve.tensor_copy(parts[:, 1, 1, :], res).then_inc(split_q, 1)
                dve.wait_ge(split_q, 3 * k + 2)
                dve.tensor_tensor(parts[:, 1, 2, :], res, parts[:, 1, 1, :], ALU.subtract).then_inc(split_q, 1)

            def dense(item):
                name, k, c = item
                layer, b = chain_of_job_layers(k)
                n = USE[item]
                if name == "ADA0":
                    dve.wait_ge(tile_full, n + 1)
                    settle(dve.tensor_tensor(modv[:, 0:4, :], bank(n)[:, 0:8].rearrange("p (m b) -> p m b", b=NB),
                                             vec[:, V_BIAS:V_BIAS + 4].unsqueeze(2).to_broadcast([P, 4, NB]), ALU.add))
                    dve.tensor_tensor(modv[:, 0:4, :], modv[:, 0:4, :],
                                      vec[:, V_ONE:V_ONE + 4].unsqueeze(2).to_broadcast([P, 4, NB]), ALU.add).then_inc(mod_ready, 1)
                    dve.wait_ge(silu_exp, 1)
                    settle(dve.tensor_scalar(silu[:, 1, :], silu[:, 0, :], 1.0, None, ALU.add))
                    settle(dve.reciprocal(silu[:, 2, :], silu[:, 1, :]))
                    dve.tensor_tensor(silu[:, 3, :], silu[:, 2, :], cond[:, :], ALU.mult).then_inc(cond_ready, 1)
                    dve.tensor_copy(ident_bf[:, :], ident[:, :]).then_inc(cond_ready, 1)
                    dve.wait_ge(cond_ready, 2)
                    dve.tensor_copy(cwide[:, 0:2, :], cond[:, :].unsqueeze(2).to_broadcast([P, NB, P]))
                    dve.tensor_copy(cwide[:, 2:4, :], silu[:, 3, :].unsqueeze(2).to_broadcast([P, NB, P])).then_inc(cond_ready, 1)
                    dve.memset(q_stack[:, 0].rearrange("p h s -> p (h s)").bitcast(F32), 0.0).then_inc(q_zero[0], 1)
                elif name == "ADA1":
                    dve.wait_ge(tile_full, n + 1)
                    settle(dve.tensor_tensor(modv[:, 4:14, :], bank(n)[:, 0:20].rearrange("p (m b) -> p m b", b=NB),
                                             vec[:, V_BIAS + 4:V_BIAS + 14].unsqueeze(2).to_broadcast([P, 10, NB]), ALU.add))
                    dve.tensor_tensor(modv[:, 4:14, :], modv[:, 4:14, :],
                                      vec[:, V_ONE + 4:V_ONE + 14].unsqueeze(2).to_broadcast([P, 10, NB]), ALU.add).then_inc(mod_ready, 1)
                elif name == "GATE":
                    dve.wait_ge(gates_full, 1)
                    dve.wait_ge(rows_in, 16)
                    for r in range(3):
                        ins = dve.tensor_tensor(gate[:, r].rearrange("p g b d -> p g b d"),
                                                exp_ps[:, r, :].rearrange("p (g b d) -> p g b d", g=2, b=NB),
                                                rows[:, 2 * r * D:2 * (r + 1) * D].rearrange("p (g d) -> p g d", g=2).unsqueeze(2).to_broadcast([P, 2, NB, D]),
                                                ALU.add)
                    ins.then_inc(gates_ready, 1)
                elif name == "ST":
                    dve.wait_ge(x_in[k], 16)
                    for t in range(T):
                        ins = dve.bn_stats(bst[:, b, t, :], x[:, b, t, :])
                    settle(ins)
                    statistics(b, k, EPS[0])
                    if k == 0:
                        dve.memset(v_ones[:, 0], 0.0).then_inc(v_set[0], 1)
                        dve.wait_ge(v_set[0], 1)
                        dve.memset(v_ones[:, 0, :, :, HD:HD + 1], 1.0).then_inc(v_set[0], 1)
                elif name == "MK":
                    i = NORM_NO[(k, 1)]
                    dve.wait_ge(late_in, LATE)
                    dve.wait_ge(h_ready, i + 1)
                    if b == 0:
                        settle(dve.tensor_copy(mask_col[:, :, :], mask_u8))
                    dve.tensor_tensor(hT[:, i % 2, :], hT[:, i % 2, :], mask_row[:, b, :], ALU.mult).then_inc(h_masked, 1)
                elif name in ("RK", "RQ"):
                    m = 0 if name == "RK" else 1
                    r = 2 * (k - NB) + m
                    sin = rot1[:, b, 0, :] if layer == 1 else rot2[:, 0, :]
                    dve.wait_ge(tile_full, n + 1)
                    if k == NB:
                        dve.wait_ge(sincos, 1)
                        dve.wait_ge(late_in, LATE)
                    col = (V_TK if name == "RK" else V_TQ)[layer]
                    settle(dve.scalar_tensor_tensor(out=work[:, 4 + m, :], in0=bank(n), scalar=vec[:, col:col + 1], in1=sin,
                                                    op0=ALU.add, op1=ALU.mult))
                    dve.wait_ge(cos_done, r + 1)
                    dve.tensor_tensor(work[:, m, :], work[:, 2 + m, :], work[:, 4 + m, :], ALU.add).then_inc(roped, 1)
                elif name == "SQ":
                    if layer == 0:
                        dve.wait_ge(qk_ready, 2 * k + 2)
                    else:
                        dve.wait_ge(roped, 2 * (k - NB) + 2)
                    if k > 0:
                        dve.wait_ge(stacked_q[(k - 1) % 2], q_rows_copied(k - 1))
                    split(k, work[:, 1, :], work[:, 5, :])
                elif name == "OG":
                    g = k % GROUPS
                    src = bank(n).rearrange("p (t j e) -> p t j e", t=T, j=4)
                    dve.wait_ge(tile_full, n + 1)
                    if k > 0:
                        dve.wait_ge(o_ready, k)
                    settle(dve.reciprocal(rden[:, :, :], src[:, :, :, HD]))
                    dve.tensor_tensor(o_tok[:, :, 32 * g:32 * g + 32].rearrange("p t (j d) -> p t j d", d=HD), src[:, :, :, 0:HD],
                                      rden[:, :, :].unsqueeze(3).to_broadcast([P, T, 4, HD]), ALU.mult).then_inc(o_ready, 1)
                elif name == "SX":
                    if c == 0:
                        dve.wait_ge(*x_written["WO", k, 0])
                        for t in range(T):
                            ins = dve.bn_stats(bst[:, b, t, :], x[:, b, t, :])
                        settle(ins)
                    statistics(b, NORM_NO[(k, c)], EPS[layer - 1] if c == 0 else EPS[layer])
                elif name == "XH":
                    i = NORM_NO[(k, c)]
                    dve.wait_ge(rstd_ready, i + 1)
                    for t in range(T):
                        ins = dve.tensor_scalar(xhat[:, i % 2, t, :], x[:, b, t, :], mv[:, i % 2, t, 0:1], rstd[:, i % 2, t:t + 1],
                                                ALU.subtract, ALU.mult)
                        ins.then_inc(xhat_ready, 1)
                elif name == "WO":
                    src = bank(n).rearrange("p (t d) -> p t d", t=T)
                    dve.wait_ge(tile_full, n + 1)
                    if (name, k) in GATED_NO:
                        r, gi = GATE_OF[(name, layer)]
                        g_tile = gate[:, r, gi, b, :].unsqueeze(1).to_broadcast([P, T, D])
                        dve.tensor_tensor(gated[:, :, :], src, g_tile, ALU.mult).then_inc(res_read, 1)
                        dve.wait_ge(res_read, residual_no[(name, k, 0)])
                        dve.wait_ge(xg_ready, GATED_NO[(name, k)] + 1)
                        dve.tensor_tensor(x[:, b], gated[:, :, :], xg[:, b], ALU.add).then_inc(x_ready, 1)
                    else:
                        dve.tensor_tensor(x[:, b], src, x[:, b], ALU.add).then_inc(res_read, 1)
                elif name[:2] == "W2":
                    is_gated = (name, k) in GATED_NO
                    if is_gated:
                        r, gi = GATE_OF[(name, layer)]
                        dve.wait_ge(xg_ready, GATED_NO[(name, k)] + 1)
                    for step in range(T + 2):
                        t = step
                        if t < T:
                            dve.wait_ge(tile_full, n + t + 1)
                            if is_gated:
                                dve.tensor_tensor(gated[:, t, :], bank(n + t)[:, 0:D], gate[:, r, gi, b, :], ALU.mult).then_inc(res_read, 1)
                            else:
                                dve.tensor_tensor(x[:, b, t, :], bank(n + t)[:, 0:D], x[:, b, t, :], ALU.add).then_inc(res_read, 1)
                        t = step - 1
                        if is_gated and 0 <= t < T:
                            dve.wait_ge(res_read, residual_no[(name, k, t)])
                            if name == "W2S":
                                ins = dve.scalar_tensor_tensor(out=x[:, b, t, :], in0=gated[:, t, :], scalar=mask_col[:, b, t:t + 1],
                                                               in1=xg[:, b, t, :], op0=ALU.mult, op1=ALU.add)
                            else:
                                ins = dve.tensor_tensor(x[:, b, t, :], gated[:, t, :], xg[:, b, t, :], ALU.add)
                            if name != "W2F":
                                ins.then_inc(x_ready, 1)
                            elif t == T - 1:
                                ins.then_inc(y_ready, 1)
                        t = step - 2 if is_gated else step - 1
                        if name != "W2F" and 0 <= t < T:
                            dve.wait_ge(*x_written[name, k, t])
                            ins = dve.bn_stats(bst[:, b, t, :], x[:, b, t, :])
                            if t == T - 1:
                                settle(ins)

            dve.memset(half[:, 4:5], 0.0).then_inc(zeros_set, 1)
            dve.memset(half[:, 0:T], -0.5).then_inc(id_ready, 1)
            dve.memset(ones_rows[:, :], 1.0).then_inc(ones_tile_set, 1)

            for s, i, items in walk():
                if i == 0 and max_rows_of(s) is not None:
                    G = max_rows_of(s)
                    m, r, pt = mx[:, G % 2], mres[:, G % 2], mparts[:, G % 2]
                    dve.wait_ge(*read_of[USE[("max", s - 1, 3)]])
                    settle(dve.tensor_scalar(pt[:, :, 0, :], m, -1.0, None, ALU.mult))
                    dve.scalar_tensor_tensor(out=r, in0=m, scalar=-1.0, in1=pt[:, :, 0, :], op0=ALU.mult, op1=ALU.subtract)
                    settle(dve.scalar_tensor_tensor(out=pt[:, :, 1, :], in0=m, scalar=-1.0, in1=pt[:, :, 0, :], op0=ALU.mult, op1=ALU.subtract))
                    dve.tensor_tensor(pt[:, :, 2, :], r, pt[:, :, 1, :], ALU.subtract).then_inc(max_split, 1)
                if maxima_of(s):
                    q, h = maxima_of(s)
                    G, n = GROUPS * q + h // 4, USE[("max", s, i)]
                    dve.wait_ge(tile_full, n + 1)
                    dve.tensor_reduce(mx[:, G % 2, i, h % 4:h % 4 + 1], ring_ps[:, n % TILES, :], AX_X, ALU.max).then_inc(tile_free, 1)
                for item in items:
                    dense(item)

        @block.gpsimd
        def _(pool):
            steps = [0]

            def settle(ins):
                steps[0] += 1
                ins.then_inc(pool_step, 1)
                pool.wait_ge(pool_step, steps[0])

            def inv_std(i):
                pool.wait_ge(stats_ready, i + 1)
                pool.tensor_tensor(rstd[:, i % 2, :], var_eps[:, i % 2, :], half[:, 0:T], ALU.pow).then_inc(rstd_ready, 1)

            def add_bias(step, k):
                layer, b = chain_of_job_layers(k)
                r, gi = GATE_OF[(step, layer)]
                gb = gate_b[:, r, gi, b, :]
                if step == "W2S":
                    for t in range(T):
                        pool.wait_ge(h_masked, b + 1)
                        ins = pool.tensor_scalar(xg[:, b, t, :], gb, mask_col[:, b, t:t + 1], 1.0, ALU.mult, ALU.mult)
                    settle(ins)
                    pool.tensor_tensor(xg[:, b], xg[:, b], x[:, b], ALU.add).then_inc(xg_ready, 1)
                else:
                    pool.tensor_tensor(xg[:, b], x[:, b], gb.unsqueeze(1).to_broadcast([P, T, D]), ALU.add).then_inc(xg_ready, 1)

            def split(k, src, res):
                pool.tensor_scalar(parts[:, 0, 0, :], src, 1.0, 1.0, ALU.mult, ALU.mult).then_inc(split_k, 1)
                pool.wait_ge(split_k, 3 * k + 1)
                settle(pool.tensor_tensor(res, src, parts[:, 0, 0, :], ALU.subtract))
                pool.tensor_scalar(parts[:, 0, 1, :], res, 1.0, 1.0, ALU.mult, ALU.mult).then_inc(split_k, 1)
                pool.wait_ge(split_k, 3 * k + 2)
                pool.tensor_tensor(parts[:, 0, 2, :], res, parts[:, 0, 1, :], ALU.subtract).then_inc(split_k, 1)

            def dense(item):
                name, k, c = item
                layer, b = chain_of_job_layers(k)
                if name == "RED":
                    bb, f = k // 2, k % 2
                    out = rot1[:, bb, f, :]
                    magic = 12582912.0
                    two_pi_hi = 6.28125
                    two_pi_lo = float(2 * np.pi - 6.28125)
                    pi = 3.1415925
                    pool.wait_ge(ang_read, bb + 1)
                    settle(pool.tensor_scalar(turns, ang[:, bb, :], float(1 / (2 * np.pi)), 0.25 * f, ALU.mult, ALU.add))
                    settle(pool.tensor_scalar(turns, turns, magic, magic, ALU.add, ALU.subtract))
                    settle(pool.tensor_scalar(out, turns, -two_pi_hi, 1.0, ALU.mult, ALU.mult))
                    settle(pool.tensor_tensor(out, out, ang[:, bb, :], ALU.add))
                    settle(pool.tensor_scalar(turns, turns, -two_pi_lo, float(np.pi / 2) * f, ALU.mult, ALU.add))
                    settle(pool.tensor_tensor(out, out, turns, ALU.add))
                    pool.tensor_scalar(out, out, pi, -pi, ALU.min, ALU.max).then_inc(ang_ready, 1)
                    pool.wait_ge(ang_ready, k + 1)
                elif name == "ST":
                    if k == 0:
                        pool.wait_ge(id_ready, 1)
                    inv_std(k)
                elif name == "GATE":
                    pool.wait_ge(gates_ready, 1)
                    settle(pool.tensor_tensor(rows[:, 10 * D:11 * D], rows[:, 10 * D:11 * D], rows[:, 11 * D:12 * D], ALU.add))
                    for r in range(3):
                        for gi in range(2):
                            col = (6 + 2 * r + gi) if (r, gi) != (2, 1) else 12
                            ins = pool.tensor_tensor(gate_b[:, r, gi], gate[:, r, gi],
                                                     rows[:, col * D:(col + 1) * D].unsqueeze(1).to_broadcast([P, NB, D]), ALU.mult)
                    ins.then_inc(gate_b_ready, 1)
                elif name == "XG0":
                    pool.wait_ge(gate_b_ready, 1)
                    for bb in range(NB):
                        pool.wait_ge(x_in[bb], 16)
                    add_bias("WO", 2)
                    add_bias("WO", 3)
                    pool.wait_ge(late_in, LATE)
                    pool.tensor_copy(pos_f[:, :, :], pos_i[:, :, :]).then_inc(pos_ready, 1)
                elif name in ("K", "Q") and layer > 0:
                    m = 0 if name == "K" else 1
                    cos = rot1[:, b, 1, :] if layer == 1 else rot2[:, 1, :]
                    if k == NB and m == 0:
                        pool.wait_ge(sincos, 1)
                        pool.wait_ge(late_in, LATE)
                    pool.wait_ge(qk_ready, 2 * k + 1 + m)
                    pool.tensor_tensor(work[:, 2 + m, :], work[:, m, :], cos, ALU.mult).then_inc(cos_done, 1)
                elif name == "RK" or (name == "K" and layer == 0):
                    if layer == 0:
                        pool.wait_ge(qk_ready, 2 * k + 1)
                    else:
                        pool.wait_ge(roped, 2 * (k - NB) + 1)
                    if k > 0:
                        pool.wait_ge(stacked_k[(k - 1) % 2], STACK_K * ((k - 1) // 2 + 1))
                    split(k, work[:, 0, :], work[:, 4, :])
                elif name == "SX":
                    inv_std(NORM_NO[(k, c)])
                    if next_gated(k, c):
                        add_bias(*next_gated(k, c))

            pool.memset(k_stack[:, 0].rearrange("p h s -> p (h s)").bitcast(F32), 0.0).then_inc(k_zero[0], 1)
            for s, i, items in walk():
                for item in items:
                    dense(item)
                    if item[0] == "ST" and item[1] == 1:
                        pool.wait_ge(v_set[1], 1)
                        pool.memset(v_ones[:, 1, :, :, HD:HD + 1], 1.0).then_inc(v_set[1], 1)


def lay_out(a):
    f = np.float32

    def vecs(*cols):
        return [np.asarray(c, f).reshape(-1, P) for c in cols]

    def heads_inner(m):
        return m.reshape(m.shape[:-1] + (H, HD)).swapaxes(-1, -2).reshape(m.shape)

    def layer(wq, wk, wv, wo, w1, w2):
        return np.concatenate([heads_inner(wq), heads_inner(wk), wv, wo, w1, rows_by_tile(w2)], 1)

    def turned(m, layer):
        return heads_inner(m)[..., [partner(d, layer) * H + h for d in range(HD) for h in range(H)]]

    def partner(d, layer):
        return (d + 2 if d % 4 < 2 else d - 2) if layer == 1 else (d + 1 if d % 2 == 0 else d - 1)

    def rows_by_tile(m):
        return m.reshape(-1, P, m.shape[1]).transpose(1, 0, 2).reshape(P, -1)

    b0, b1, b3, b3f = a["L0_cond_b_ada"], a["L1_cond_ada_b"], a["L3_cond_ada_b"], a["L3_cond_ffada_b"]
    zero, one = np.zeros(P, f), np.ones(P, f)
    qkv_w, qkv_b = a["L1_cond_qkv_w"], a["L1_cond_qkv_b"]
    shift_scale = [b[c * D:(c + 1) * D] for b, cs in ((b0, (0, 1, 3, 4)), (b1, (0, 1, 3, 4))) for c in cs]
    shift_scale += [zero, zero] + [b[c * D:(c + 1) * D] for b in (b3, b3f) for c in (0, 1)]
    ones = [one if m % 2 == 1 and m != 9 else zero for m in range(MOD)]
    vec = vecs(*shift_scale, *ones,
               heads_inner(a["L0_cond_bq"]), heads_inner(a["L0_cond_bk"]), a["L0_cond_bv"],
               heads_inner(qkv_b[0:D]), heads_inner(qkv_b[D:2 * D]), qkv_b[2 * D:],
               a["L0_cond_b1"], a["L1_cond_fc1_b"], a["L2_cond_mlp_ln_scale"], a["L3_cond_ssm_b1"], a["L3_cond_bwd_b1"],
               a["L3_cond_ff_b1"], turned(qkv_b[0:D], 1), turned(qkv_b[D:2 * D], 1))
    vec = np.concatenate(vec, 0)
    pad = np.zeros((V_N - len(vec), P), f)
    vec = np.concatenate([vec, pad], 0).T
    ada = np.concatenate([a["L0_cond_W_ada"], a["L1_cond_ada_w"], a["L2_cond_w_offset"], a["L2_cond_w_scale"],
                          a["L3_cond_ada_w"], a["L3_cond_ffada_w"]], 1)
    gates = [b0[2 * D:3 * D], b0[5 * D:], b1[2 * D:3 * D], b1[5 * D:], b3[2 * D:], b3f[2 * D:]]
    rows = np.concatenate(gates + [a["L0_cond_bo"], a["L0_cond_b2"], a["L1_cond_proj_b"], a["L1_cond_fc2_b"],
                                   a["L3_cond_ssm_b2"], a["L3_cond_bwd_b2"], a["L3_cond_ff_b2"]])[None, :]
    freq = np.zeros((2, P), f)
    inv1 = (f(1.0) / f(100.0) ** (np.arange(0, 4, 2, dtype=f) / f(4))).astype(f)
    inv2 = (f(10000.0) ** (-np.arange(0, HD, 2, dtype=f) / f(HD))).astype(f)
    grid = np.arange(S, dtype=f)[:, None] * inv2[None, :]
    rot2 = np.zeros((P, 2, S), f)
    for d in range(HD):
        for h in range(H):
            to = d * H + h
            freq[d // 4, to] = inv1[d % 2] * (-1 if d % 4 < 2 else 1)
            sign = -1 if d % 2 == 0 else 1
            rot2[to, 0], rot2[to, 1] = sign * np.sin(grid[:, d // 2].astype(np.float64)), np.cos(grid[:, d // 2].astype(np.float64))
    mask = a["mask_BxS_bk0"].view(np.uint8)
    return {
        "x": a["x"], "cond": a["cond_1024"].T, "vec": vec, "ident": np.eye(P, dtype=f), "ada": ada, "rows": rows,
        "freq": freq, "rot2": rot2,
        "pos": a["itok_BxSx2_0_63"].transpose(2, 0, 1), "mask_row": mask.view(np.int32),
        "mask_col": np.ascontiguousarray(mask.reshape(NB, T, P).transpose(2, 0, 1)).reshape(P, NB * T).view(np.int32),
        "w0": layer(*[a["L0_cond_" + n] for n in ("Wq", "Wk", "Wv", "Wo", "W1", "W2")]),
        "w1": np.concatenate([layer(qkv_w[:, 0:D], qkv_w[:, D:2 * D], qkv_w[:, 2 * D:], a["L1_cond_proj_w"], a["L1_cond_fc1_w"],
                                    a["L1_cond_fc2_w"]), turned(qkv_w[:, 0:D], 1), turned(qkv_w[:, D:2 * D], 1)], 1),
        "w2": np.concatenate([layer(*[a["L2_cond_" + n] for n in ("wq", "wk", "wv", "wo", "w1", "w2")]),
                              turned(a["L2_cond_wq"], 2), turned(a["L2_cond_wk"], 2)], 1),
        "w3": np.concatenate([a["L3_cond_ssm_w1"], a["L3_cond_bwd_w1"], a["L3_cond_ssm_w2"], a["L3_cond_bwd_w2"],
                              a["L3_cond_ff_w1"], rows_by_tile(a["L3_cond_ff_w2"])], 1),
    }


def kernel(**inputs):
    import concourse.bacc as bacc
    from concourse.bass_utils import run_bass_kernel_spmd

    nc = bacc.Bacc("TRN2", target_bir_lowering=False, num_devices=1)
    arrays, ins = {}, {}
    for name, a in lay_out({n: np.asarray(v) for n, v in inputs.items()}).items():
        a = np.ascontiguousarray(a)
        arrays[f"in_{name}_dram"] = a
        ins[name] = nc.dram_tensor(f"in_{name}_dram", a.shape, mybir.dt.from_np(a.dtype), kind="ExternalInput").ap()
    y = nc.dram_tensor("out_0_dram", (NB, S, D), F32, kind="ExternalOutput").ap()
    build(nc, ins, y)
    r = run_bass_kernel_spmd(nc, [arrays], core_ids=[0])
    return r.results[0]["out_0_dram"]
```
